# Optimizing a Trainium2 kernel written in Bass

```python
import numpy as np
import jax
import jax.numpy as jnp

def _softmax(x, axis=-1):
    return jax.nn.softmax(x, axis=axis)

def _gelu(x):
    return jax.nn.gelu(x, approximate=True)

def _silu(x):
    return jax.nn.silu(x)

def _sigmoid(x):
    return jax.nn.sigmoid(x)

def _layernorm(x, axis=-1, eps=1e-05):
    m = jnp.mean(x, axis=axis, keepdims=True)
    v = jnp.var(x, axis=axis, keepdims=True)
    return (x - m) / jnp.sqrt(v + eps)

def _scatter_add(tgt, idx, src, axis=0):
    return tgt.at[idx].add(src)

def _segment_sum(src, seg, n):
    return jax.ops.segment_sum(src, seg, n)
kernel_name = 'mk_hybrid_d1_jaxref_r4_0cc6c8'

def setup_inputs(seed: int=0):
    np.random.seed(seed)
    _w = jnp.asarray

    def _L0_attn_a_setup():
        import jax, jax.numpy as jnp
        import numpy as np
        B, T, HID = (1, 512, 512)
        H = 16
        D = HID // H
        EPS = 1e-05

        def _layer_norm(x, eps=1e-05):
            mu = jnp.mean(x, axis=-1, keepdims=True)
            var = jnp.mean((x - mu) ** 2, axis=-1, keepdims=True)
            return (x - mu) * jax.lax.rsqrt(var + eps)

        def _feature_map(x, gamma, beta):
            return _layer_norm(x * gamma + beta)
        key = jax.random.key(seed)
        ks = jax.random.split(key, 8)
        s = HID ** (-0.5)
        return {'hidden_states': jax.random.normal(ks[0], (B, T, HID), jnp.float32), 'Wq': jax.random.normal(ks[1], (HID, HID), jnp.float32) * s, 'Wk': jax.random.normal(ks[2], (HID, HID), jnp.float32) * s, 'Wv': jax.random.normal(ks[3], (HID, HID), jnp.float32) * s, 'Wo': jax.random.normal(ks[4], (HID, HID), jnp.float32) * s, 'gamma': 1.0 + 0.1 * jax.random.normal(ks[5], (D,), jnp.float32), 'beta': 0.1 * jax.random.normal(ks[6], (D,), jnp.float32)}
    _L0_attn_a_in = _L0_attn_a_setup()

    def _L0_attn_b_setup():
        import jax, jax.numpy as jnp
        import numpy as np
        D_MODEL = 512
        HEADS = 16
        HEAD_DIM = D_MODEL // HEADS
        key = jax.random.key(seed)
        k1, k2, k3 = jax.random.split(key, 3)
        B, S = (1, 512)
        x = jax.random.normal(k1, (B, S, D_MODEL), dtype=jnp.float32)
        Wqkv_w = jax.random.normal(k2, (D_MODEL + 2 * HEAD_DIM, D_MODEL), dtype=jnp.float32) * D_MODEL ** (-0.5)
        Wqkv_b = jnp.zeros((D_MODEL + 2 * HEAD_DIM,), dtype=jnp.float32)
        out_w = jax.random.normal(k3, (D_MODEL, D_MODEL), dtype=jnp.float32) * D_MODEL ** (-0.5)
        out_b = jnp.zeros((D_MODEL,), dtype=jnp.float32)
        return {'x': x, 'Wqkv_w': Wqkv_w, 'Wqkv_b': Wqkv_b, 'out_w': out_w, 'out_b': out_b}
    _L0_attn_b_in = _L0_attn_b_setup()

    def _L0_ffn_setup():
        import jax, jax.numpy as jnp
        import numpy as np
        import math
        N_EMBD = 512
        N_HEAD = 16
        HEAD_DIM = N_EMBD // N_HEAD
        B, T = (2, 512)
        key = jax.random.key(seed)
        k1, k2, k3 = jax.random.split(key, 3)
        x = jax.random.normal(k1, (B, T, N_EMBD), dtype=jnp.float32)
        W_gate = jax.random.normal(k2, (N_HEAD, N_EMBD), dtype=jnp.float32) * 0.02
        W_qkv = jax.random.normal(k3, (3 * N_EMBD, N_EMBD), dtype=jnp.float32) * 0.02
        return {'x': x, 'W_gate': W_gate, 'W_qkv': W_qkv}
    _L0_ffn_in = _L0_ffn_setup()
    _d = {'L0_attn_a_hidden_states': _L0_attn_a_in['hidden_states'], 'L0_attn_a_Wq': _L0_attn_a_in['Wq'], 'L0_attn_a_Wk': _L0_attn_a_in['Wk'], 'L0_attn_a_Wv': _L0_attn_a_in['Wv'], 'L0_attn_a_Wo': _L0_attn_a_in['Wo'], 'L0_attn_a_gamma': _L0_attn_a_in['gamma'], 'L0_attn_a_beta': _L0_attn_a_in['beta'], 'L0_attn_b_Wqkv_w': _L0_attn_b_in['Wqkv_w'], 'L0_attn_b_Wqkv_b': _L0_attn_b_in['Wqkv_b'], 'L0_attn_b_out_w': _L0_attn_b_in['out_w'], 'L0_attn_b_out_b': _L0_attn_b_in['out_b'], 'L0_ffn_W_gate': _L0_ffn_in['W_gate'], 'L0_ffn_W_qkv': _L0_ffn_in['W_qkv']}
    _x0 = _d['L0_attn_a_hidden_states']
    _d['L0_attn_a_hidden_states'] = jax.random.normal(jax.random.fold_in(jax.random.key(seed), 1), (4, 1024, 512), dtype=_x0.dtype)
    del _x0
    return _d

def reference(L0_attn_a_hidden_states, L0_attn_a_Wq, L0_attn_a_Wk, L0_attn_a_Wv, L0_attn_a_Wo, L0_attn_a_gamma, L0_attn_a_beta, L0_attn_b_Wqkv_w, L0_attn_b_Wqkv_b, L0_attn_b_out_w, L0_attn_b_out_b, L0_ffn_W_gate, L0_ffn_W_qkv):

    def _L0_attn_a_ref(hidden_states, Wq, Wk, Wv, Wo, gamma, beta):
        import jax, jax.numpy as jnp
        import numpy as np
        B, T, HID = (1, 512, 512)
        H = 16
        D = HID // H
        EPS = 1e-05

        def _layer_norm(x, eps=1e-05):
            mu = jnp.mean(x, axis=-1, keepdims=True)
            var = jnp.mean((x - mu) ** 2, axis=-1, keepdims=True)
            return (x - mu) * jax.lax.rsqrt(var + eps)

        def _feature_map(x, gamma, beta):
            return _layer_norm(x * gamma + beta)
        b, t, _ = hidden_states.shape
        q = (hidden_states @ Wq.T).reshape(b, t, H, D)
        k = (hidden_states @ Wk.T).reshape(b, t, H, D)
        v = (hidden_states @ Wv.T).reshape(b, t, H, D)
        q = _feature_map(q, gamma, beta)
        k = _feature_map(k, gamma, beta)
        q = q * D ** (-0.5)
        attn = jnp.einsum('bqhd,bkhd->bhqk', q, k) ** 2
        mask = jnp.tril(jnp.ones((t, t), dtype=bool))
        attn = jnp.where(mask, attn, 0.0)
        o = jnp.einsum('bhqk,bkhd->bqhd', attn, v)
        z = jnp.sum(attn, axis=-1)
        o = o / (jnp.swapaxes(z, 1, 2)[..., None] + EPS)
        o = o.reshape(b, t, H * D)
        return o @ Wo.T

    def _L0_attn_b_ref(x, Wqkv_w, Wqkv_b, out_w, out_b):
        import jax, jax.numpy as jnp
        import numpy as np
        D_MODEL = 512
        HEADS = 16
        HEAD_DIM = D_MODEL // HEADS
        B, S, _ = x.shape
        qkv = jnp.einsum('bsd,ed->bse', x, Wqkv_w) + Wqkv_b
        q = qkv[..., :D_MODEL]
        k = qkv[..., D_MODEL:D_MODEL + HEAD_DIM]
        v = qkv[..., D_MODEL + HEAD_DIM:]
        q = q.reshape(B, S, HEADS, HEAD_DIM)
        scale = 1.0 / np.sqrt(HEAD_DIM)
        scores = jnp.einsum('bqhd,bkd->bhqk', q, k) * scale
        min_val = jnp.finfo(scores.dtype).min
        causal = jnp.tril(jnp.ones((S, S), dtype=bool))
        scores = jnp.where(causal[None, None], scores, min_val)
        attn = jax.nn.softmax(scores, axis=-1)
        ctx = jnp.einsum('bhqk,bkd->bqhd', attn, v)
        ctx = ctx.reshape(B, S, D_MODEL)
        out = jnp.einsum('bsd,ed->bse', ctx, out_w) + out_b
        return out

    def _L0_ffn_ref(x, W_gate, W_qkv):
        import jax, jax.numpy as jnp
        import numpy as np
        import math
        N_EMBD = 512
        N_HEAD = 16
        HEAD_DIM = N_EMBD // N_HEAD
        B, T = (2, 512)
        Bb, Tt, C = x.shape
        H, hd = (N_HEAD, HEAD_DIM)
        gating = jax.nn.softmax(x @ W_gate.T, axis=-1)
        idx = jnp.argmax(gating, axis=-1)
        indicator = jax.nn.one_hot(idx, H, dtype=gating.dtype)
        top1_val = jnp.max(gating, axis=-1, keepdims=True)
        gating_top1 = indicator * top1_val
        qkv = x @ W_qkv.T
        q, k, v = jnp.split(qkv, 3, axis=-1)
        k = k.reshape(Bb, Tt, H, hd)
        v = v.reshape(Bb, Tt, H, hd)
        k_shared = jnp.einsum('bth,bthd->btd', indicator, k)
        v_shared = jnp.einsum('bth,bthd->btd', gating_top1, v)
        q = q.reshape(Bb, Tt, H, hd).transpose(0, 2, 1, 3)
        att = jnp.einsum('bhqd,bkd->bhqk', q, k_shared) * (1.0 / math.sqrt(hd))
        causal = jnp.tril(jnp.ones((Tt, Tt), dtype=bool))
        att = jnp.where(causal[None, None, :, :], att, -jnp.inf)
        att = jax.nn.softmax(att, axis=-1)
        y = jnp.einsum('bhqk,bkd->bhqd', att, v_shared)
        y = y.transpose(0, 2, 1, 3).reshape(Bb, Tt, C)
        return y
    x = L0_attn_a_hidden_states
    x = x + _L0_attn_a_ref(_layernorm(x, axis=-1), L0_attn_a_Wq, L0_attn_a_Wk, L0_attn_a_Wv, L0_attn_a_Wo, L0_attn_a_gamma, L0_attn_a_beta)
    x = x + _L0_ffn_ref(_layernorm(x, axis=-1), L0_ffn_W_gate, L0_ffn_W_qkv)
    x = x + _L0_attn_b_ref(_layernorm(x, axis=-1), L0_attn_b_Wqkv_w, L0_attn_b_Wqkv_b, L0_attn_b_out_w, L0_attn_b_out_b)
    x = x + _L0_ffn_ref(_layernorm(x, axis=-1), L0_ffn_W_gate, L0_ffn_W_qkv)
    return x

_drawn_inputs = setup_inputs


def setup_inputs(seed=0):
    import zlib

    import numpy as np

    out = dict(_drawn_inputs(seed))
    spreads = {'L0_attn_b_Wqkv_b': (0.0, 0.1), 'L0_attn_b_out_b': (0.0, 0.1)}
    factors = {}
    for name, (base, spread) in spreads.items():
        noise = np.random.default_rng([zlib.crc32(name.encode()), seed]).standard_normal(out[name].shape)
        drawn = base * np.exp(spread * noise) if base else spread * noise
        out[name] = jnp.asarray(drawn.astype(out[name].dtype))
    for name, factor in factors.items():
        out[name] = (out[name] * factor).astype(out[name].dtype)
    return out
```

```python
from contextlib import ExitStack

import concourse.bass as bass
from concourse import mybir

F32 = mybir.dt.float32
F32R = mybir.dt.float32r
BF16 = mybir.dt.bfloat16
ALU = mybir.AluOpType
ACT = mybir.ActivationFunctionType
AX_X = mybir.AxisListType.X

P = 128
B, T, C = 4, 1024, 512
HEADS, D = 16, 32
HG = P // D
NG = HEADS // HG
KC = C // P
NT = T // P
CHUNK = 512
NC = T // CHUNK
TPC = CHUNK // P
EPS = 1e-5
SCALE = float(D) ** -0.5
MASKED = -1.0e30
LOWEST = -3.0e38
HIGH, LOW = 0, 1
PAIRS = ((HIGH, HIGH), (HIGH, LOW), (LOW, HIGH))
QUERY_ROWS = (HIGH, LOW, HIGH)
KEY_ROWS = (HIGH, HIGH, LOW)
STACK = 3 * D
SHIFT = STACK + 2
DMA = 16
LAYERS = ("squared", "gated", "mqa", "gated")

STEPS = [(c, kb) for c in range(NC) for kb in range(TPC * (c + 1))]
NSTEPS = len(STEPS)
PIECES = [(t, i, p) for t in range(NT) for i in range(HG) for p in range(t // TPC + 1)]
NPIECES = len(PIECES)
FIRST_PIECE_STEP, PIECES_PER_STEP = 3, 7
NEXT_SOFTMAX = {0: ("q", 0), 1: ("q", 1), NSTEPS - 2: ("max",)}
NEXT_SQUARED = {0: ("v", 0), 1: ("v", 1), 2: ("q", 0), 3: ("qvar", 0), 4: ("q", 1), 5: ("qvar", 1),
                6: ("k", 0), 7: ("kvar", 0), 8: ("k", 1), 9: ("kvar", 1)}


def pieces_at(step, late):
    a = (step - FIRST_PIECE_STEP) * PIECES_PER_STEP
    if a < 0:
        return range(0)
    mid = min(a + 4, NPIECES)
    return range(mid, min(a + PIECES_PER_STEP, NPIECES)) if late else range(min(a, NPIECES), mid)


def work_units(kind):
    names = [("ln", t) for t in range(NT)]
    if kind == "mqa":
        names += [("ks", c) for c in range(NC)] + [("vs",)]
    if kind == "gated":
        names += [("gate",)] + [(w, t) for t in range(NT) for w in ("kall", "vall")]
        names += [("kt", c) for c in range(NC)]
    following = NEXT_SQUARED if kind == "squared" else NEXT_SOFTMAX
    for g in range(NG):
        names += [(u[0], g, *u[1:]) for _, u in sorted(following.items())]
    names += [("out", t) for t in range(NT)]
    return {name: n for n, name in enumerate(names)}


class Signals:

    def __init__(self, nc, ctx):
        self.all = []

        def sem(name):
            self.all.append(ctx.enter_context(nc.semaphore(name)))
            return self.all[-1]

        self.loaded = sem("loaded")
        self.built = sem("built")
        self.vector_step = sem("vector_step")
        self.scalar_step = sem("scalar_step")
        self.variance = sem("variance")
        self.rstd = sem("rstd")
        self.normed = sem("normed")
        self.work_ready = [sem(f"work_ready{k}") for k in range(2)]
        self.work_high = [sem(f"work_high{k}") for k in range(2)]
        self.work_free = [sem(f"work_free{k}") for k in range(2)]
        self.gate_shifted = sem("gate_shifted")
        self.gate_exp = sem("gate_exp")
        self.selected = sem("selected")
        self.low_done = [sem(f"low_done{k}") for k in range(2)]
        self.centred = sem("centred")
        self.stacked = [sem(f"stacked{k}") for k in range(2)]
        self.piece_ready = sem("piece_ready")
        self.piece_used = sem("piece_used")
        self.max_ready = sem("max_ready")
        self.shift_moved = sem("shift_moved")
        self.scores_ready = sem("scores_ready")
        self.probs_ready = sem("probs_ready")
        self.probs_masked = sem("probs_masked")
        self.probs_used = sem("probs_used")
        self.sums_used = sem("sums_used")
        self.residual = [sem(f"residual{k}") for k in range(4)]
        self.biased = sem("biased")
        self.stored = [sem(f"stored{k}") for k in range(4)]
        numbers = [s.num for s in self.all]
        self.range = range(min(numbers), max(numbers) + 1)
        assert len(self.range) == len(self.all)


def make_constants(nc, ctx, sg):
    def sb(name, shape, dt=F32):
        return ctx.enter_context(nc.sbuf_tensor(name, shape, dt))

    k = {
        "ident": sb("ident", [P, P]),
        "ident16": sb("ident16", [P, P], BF16),
        "mask": sb("mask", [P, P], BF16),
        "mask_t": sb("mask_t", [P, P], BF16),
        "ones": sb("ones", [P, D]),
        "head_mean": sb("head_mean", [P, HG, D]),
        "centre": sb("centre", [P, P]),
        "rank": sb("rank", [P, NT, HEADS]),
        "minus_half": sb("minus_half", [P, NT]),
        "eps": sb("eps", [P, 1]),
    }
    with nc.Block() as block:
        @block.gpsimd
        def _(pool):
            pool.memset(k["ident"][:], 0.0).then_inc(sg.built, 1)
            pool.memset(k["ident16"][:], 0.0).then_inc(sg.built, 1)
            pool.memset(k["mask"][:], 0.0).then_inc(sg.built, 1)
            pool.memset(k["mask_t"][:], 0.0).then_inc(sg.built, 1)
            pool.memset(k["ones"][:], 1.0)
            pool.memset(k["head_mean"][:], 1.0 / D).then_inc(sg.built, 1)
            pool.memset(k["minus_half"][:], -0.5)
            pool.memset(k["eps"][:], EPS)
            pool.iota(k["rank"][:], pattern=[[0, NT], [-1, HEADS]], base=HEADS, channel_multiplier=0,
                      allow_small_or_imprecise_dtypes=True)
            pool.wait_ge(sg.built, 5)
            for name in ("ident", "ident16"):
                pool.affine_select(out=k[name][:], in_=k[name][:], compare_op=ALU.not_equal, fill=1.0, base=0,
                                   pattern=[[-1, P]], channel_multiplier=1).then_inc(sg.built, 1)
            pool.affine_select(out=k["mask"][:], in_=k["mask"][:], compare_op=ALU.is_ge, fill=MASKED, base=0,
                               pattern=[[-1, P]], channel_multiplier=1)
            pool.affine_select(out=k["mask_t"][:], in_=k["mask_t"][:], compare_op=ALU.is_ge, fill=MASKED, base=0,
                               pattern=[[1, P]], channel_multiplier=-1)
            pool.affine_select(out=k["head_mean"][:], in_=k["head_mean"][:], compare_op=ALU.is_ge, fill=0.0, base=0,
                               pattern=[[-D, HG], [0, D]], channel_multiplier=1).then_inc(sg.built, 1)
            pool.wait_ge(sg.built, 8)
            pool.affine_select(out=k["head_mean"][:], in_=k["head_mean"][:], compare_op=ALU.is_ge, fill=0.0,
                               base=D - 1, pattern=[[D, HG], [0, D]], channel_multiplier=-1).then_inc(sg.built, 1)
            pool.wait_ge(sg.built, 9)
            pool.tensor_tensor(k["centre"][:], k["ident"][:], k["head_mean"][:].rearrange("p i d -> p (i d)"),
                               ALU.subtract)
    nc.all_engine_barrier(sems_to_clear=sg.range)
    return k


def load_rows(w):
    return w.rearrange("(kc p) n -> p kc n", p=P)


def prepare_squared(nc, sg, k, psum, w, dram):
    with ExitStack() as ctx:
        def sb(name, shape, dt=F32):
            return ctx.enter_context(nc.sbuf_tensor(name, shape, dt))

        raw = {n: sb(f"raw_{n}", [P, NG, C]) for n in ("wq", "wk")}
        raw_v = sb("raw_v", [P, KC, C])
        gamma, beta = sb("gamma", [P, 1]), sb("beta", [P, 1])
        scaled = sb("scaled", [P, P])
        block = ctx.enter_context(nc.Block())

        @block.sync
        def _(sp):
            for n in ("wq", "wk"):
                sp.dma_start(raw[n][:], dram[n].rearrange("(g p) c -> p g c", p=P)).then_inc(sg.loaded, DMA)
            sp.dma_start(raw_v[:], load_rows(dram["wvT"])).then_inc(sg.loaded, DMA)
            sp.dma_start(w["wo"][:], load_rows(dram["woT"])).then_inc(sg.loaded, DMA)
            for i in range(HG):
                sp.dma_start(gamma[D * i:D * i + D, :], dram["gamma"].rearrange("(d a) -> d a", a=1)).then_inc(sg.loaded, DMA)
                sp.dma_start(beta[D * i:D * i + D, :], dram["beta"].rearrange("(d a) -> d a", a=1)).then_inc(sg.loaded, DMA)

        everything = DMA * (4 + 2 * HG)

        @block.vector
        def _(dve):
            dve.wait_ge(sg.loaded, everything)
            dve.tensor_scalar(scaled[:], k["centre"][:], gamma[:, 0:1], None, ALU.mult).then_inc(sg.vector_step, 1)
            dve.wait_ge(sg.scalar_step, 1)
            dve.tensor_tensor(w["wv"][:, LOW], raw_v[:], w["wv"][:, HIGH].bitcast(F32), ALU.subtract)
            for u in range(2 * KC):
                n, kc = ("wq", "wk")[u // KC], u % KC
                dve.wait_ge(sg.scalar_step, 2 + u)
                dve.tensor_tensor(w[n][:, LOW, kc], psum["work"][:, u % 2], w[n][:, HIGH, kc].bitcast(F32),
                                  ALU.subtract).then_inc(sg.work_free[u % 2], 1)
            dve.wait_ge(sg.work_ready[0], KC + 1)
            dve.tensor_copy(w["feature_bias"][:], psum["work"][:, 0, 0:1])

        @block.scalar
        def _(act):
            act.wait_ge(sg.loaded, everything)
            act.activation(w["wv"][:, HIGH], raw_v[:], ACT.Copy).then_inc(sg.scalar_step, 1)
            for u in range(2 * KC):
                n, kc = ("wq", "wk")[u // KC], u % KC
                act.wait_ge(sg.work_ready[u % 2], u // 2 + 1)
                act.activation(w[n][:, HIGH, kc], psum["work"][:, u % 2], ACT.Copy).then_inc(sg.scalar_step, 1)

        @block.tensor
        def _(pe):
            pe.wait_ge(sg.loaded, everything)
            pe.wait_ge(sg.vector_step, 1)
            for u in range(2 * KC):
                n, kc = ("wq", "wk")[u // KC], u % KC
                if u >= 2:
                    pe.wait_ge(sg.work_free[u % 2], u // 2)
                for g in range(NG):
                    mm = pe.matmul(psum["work"][:, u % 2, P * g:P * g + P], raw[n][:, g, P * kc:P * kc + P], scaled[:],
                                   start=True, stop=True)
                mm.then_inc(sg.work_ready[u % 2], 1)
            pe.wait_ge(sg.work_free[0], KC)
            pe.matmul(psum["work"][:, 0, 0:1], k["centre"][:], beta[:], start=True, stop=True).then_inc(sg.work_ready[0], 1)
    nc.all_engine_barrier(sems_to_clear=sg.range)


def prepare_gated(nc, sg, k, psum, w, dram, layer):
    with ExitStack() as ctx:
        n_all = 3 * C
        raw = ctx.enter_context(nc.sbuf_tensor(f"raw_qkv_{layer}", [P, KC, n_all], F32))
        raw_gate = ctx.enter_context(nc.sbuf_tensor(f"raw_gate_{layer}", [P, KC, HEADS], F32))
        block = ctx.enter_context(nc.Block())
        parts = [("wq", raw[:, :, 0:C]), ("wk", raw[:, :, C:2 * C]), ("wv", raw[:, :, 2 * C:3 * C]), ("wg", raw_gate[:])]

        @block.sync
        def _(sp):
            sp.dma_start(raw[:], load_rows(dram["wqkvT"])).then_inc(sg.loaded, DMA)
            sp.dma_start(raw_gate[:], load_rows(dram["wgateT"])).then_inc(sg.loaded, DMA)

        split(block, sg, w, parts, 2 * DMA)
    nc.all_engine_barrier(sems_to_clear=sg.range)


def prepare_mqa(nc, sg, k, psum, w, dram):
    with ExitStack() as ctx:
        n_all = C + 2 * D
        raw = ctx.enter_context(nc.sbuf_tensor("raw_qkv", [P, KC, n_all], F32))
        block = ctx.enter_context(nc.Block())
        parts = [("wq", raw[:, :, 0:C]), ("wv", raw[:, :, C + D:C + 2 * D])]
        parts += [(f"wk{r}", raw[:, :, C:C + D]) for r in range(3)]

        @block.sync
        def _(sp):
            sp.dma_start(raw[:], load_rows(dram["wqkvT"])).then_inc(sg.loaded, DMA)
            sp.dma_start(w["wo"][:], load_rows(dram["woT"])).then_inc(sg.loaded, DMA)
            bias = dram["bqkv"]
            for g in range(NG):
                sp.dma_start(w["bq"][:, g:g + 1], bias[P * g:P * g + P].rearrange("(p a) -> p a", a=1)).then_inc(sg.loaded, DMA)
            for r in range(3):
                sp.dma_start(w["bk"][D * r:D * r + D, :], bias[C:C + D].rearrange("(d a) -> d a", a=1)).then_inc(sg.loaded, DMA)
            sp.dma_start(w["bv"][:], bias[C + D:C + 2 * D].partition_broadcast(P)).then_inc(sg.loaded, DMA)
            sp.dma_start(w["bo"][:], dram["bout"].partition_broadcast(P)).then_inc(sg.loaded, DMA)

        split(block, sg, w, parts, DMA * (7 + NG))
    nc.all_engine_barrier(sems_to_clear=sg.range)


def split(block, sg, w, parts, loads):
    @block.scalar
    def _(act):
        act.wait_ge(sg.loaded, loads)
        for name, raw in parts:
            act.activation(w[name][:, HIGH], raw, ACT.Copy).then_inc(sg.scalar_step, 1)

    @block.vector
    def _(dve):
        for n, (name, raw) in enumerate(parts):
            dve.wait_ge(sg.scalar_step, n + 1)
            dve.tensor_tensor(w[name][:, LOW], raw, w[name][:, HIGH].bitcast(F32), ALU.subtract)


def pair_product(pe, out, left, right):
    terms = [(kc, a, b) for kc in range(KC) for a, b in PAIRS]
    for n, (kc, a, b) in enumerate(terms):
        mm = pe.matmul(out, left(a, kc), right(b, kc), start=(n == 0), stop=(n == len(terms) - 1))
    return mm


def stage_buffers(nc, ctx, kind, layer):
    def sb(name, shape, dt=F32):
        return ctx.enter_context(nc.sbuf_tensor(f"{name}_{layer}", shape, dt))

    s = {
        "xy": sb("xy", [P, NT * C]),
        "stats": sb("stats", [P, NT, 6]),
        "mean_var": sb("mean_var", [P, NT, 2]),
        "var_eps": sb("var_eps", [P, NT]),
        "rstd": sb("rstd", [P, NT]),
        "tiles": sb("tiles", [P, 4, C]),
        "xnT": sb("xnT", [P, 2, KC, T], F32R),
        "pair": sb("pair", [P, NC, 2, CHUNK], F32R),
        "q": sb("q_stack", [P, 2, HG, T], F32R),
        "inverse": sb("inverse", [P, CHUNK]),
    }
    if kind == "squared":
        s["slots"] = 2
        s["k"] = sb("k_stack", [P, 2, HG, T], F32R)
        s["v"] = sb("v", [P, 2, NT, P])
        s["centred"] = sb("centred_heads", [P, 2, CHUNK])
        s["squares"] = sb("squares", [P, CHUNK])
        s["deviation"] = sb("deviations", [P, CHUNK])
    else:
        s["slots"] = 3
        s["k"] = sb("k_stack", [P, T], F32R)
        s["v"] = sb("v", [P, NT, D])
        s["maxima"] = sb("maxima", [P, 2, HG, NT, 2])
        s["minus_max"] = sb("minus_max", [P, 2, HG * NT])
        s["shift"] = sb("shift", [HG * NT, 2, 2, P], F32R)
    if kind == "gated":
        for name in ("logits", "gate_exp", "is_max", "chosen", "gate"):
            s[name] = sb(f"g_{name}", [P, NT, HEADS])
        for name in ("logit_max", "exp_sum", "top", "best"):
            s[name] = sb(f"g_{name}", [P, NT])
        s["masked"] = sb("masked_heads", [P, 2, C])
        s["k_token"] = sb("k_token", [P, NT, STACK])
    s["probs"] = sb("probs", [P, s["slots"], HG, CHUNK])
    return s


def stage(nc, sg, k, psum, w, s, kind, b, source, result):
    squared, gated, mqa = kind == "squared", kind == "gated", kind == "mqa"
    unit = work_units(kind)
    following = NEXT_SQUARED if squared else NEXT_SOFTMAX
    work, slots = psum["work"], s["slots"]
    pairs_made = 2 if squared else 1
    rows = STACK if squared else SHIFT
    xy = s["xy"]

    def x_tile(t):
        return xy[:, C * t:C * t + C]

    def heads_out(g, c):
        return xy[:, T * g + CHUNK * c:T * g + CHUNK * c + CHUNK]

    def tile_of(tensor, t):
        return tensor[:, P * t:P * t + P]

    def bank(name):
        return unit[name] % 2

    def wait_work(eng, name):
        eng.wait_ge(sg.work_ready[bank(name)], unit[name] // 2 + 1)

    def wait_free(eng, name):
        eng.wait_ge(sg.work_free[bank(name)], unit[name] // 2 + 1)

    def wait_high(eng, name, count):
        eng.wait_ge(sg.work_high[bank(name)], count)

    highs = {}
    seen = [0, 0]
    for name in unit:
        if name[0] in (("ln",) if squared else ("ln", "ks", "kt", "q", "max")):
            seen[bank(name)] += 1
            highs[name] = seen[bank(name)]

    def feature_unit(n, suffix=""):
        return ("qk"[n // 2 % 2] + suffix, n // 4, n % 2)

    def start(c):
        return STEPS.index((c, 0))

    with nc.Block() as block:
        @block.sync
        def _(sp):
            sp.dma_start(xy[:].rearrange("p (t c) -> p t c", t=NT),
                         source[bass.ds(b, 1), :, :].rearrange("b (t p) c -> p (b t) c", p=P)).then_inc(sg.loaded, DMA)

            def stack(g, c, target, parts, number):
                if squared:
                    sp.wait_ge(sg.low_done[c], number + 1)
                else:
                    wait_free(sp, ("q", g, c))
                for i in range(HG):
                    for r, part in enumerate(parts):
                        sp.dma_start(target[D * r:D * r + D, g % 2, i, CHUNK * c:CHUNK * c + CHUNK].bitcast(F32),
                                     s["pair"][D * i:D * i + D, c, part, :].bitcast(F32)).then_inc(sg.stacked[c], DMA)

            for g in range(NG):
                for c in range(NC):
                    stack(g, c, s["q"], QUERY_ROWS, pairs_made * g)
                if squared:
                    for c in range(NC):
                        stack(g, c, s["k"], KEY_ROWS, pairs_made * g + 1)
                else:
                    wait_free(sp, ("max", g))
                    for part in (HIGH, LOW):
                        sp.dma_start(s["q"][STACK + part:STACK + part + 1, g % 2, :, :].rearrange("a i t -> a (i t)").bitcast(F32),
                                     s["shift"][:, g % 2, part, :].bitcast(F32)).then_inc(sg.shift_moved, DMA)

            def residual(t):
                sp.dma_start(s["tiles"][:, t % 4, :],
                             source[bass.ds(b, 1), P * t:P * t + P, :].rearrange("b p c -> p (b c)")).then_inc(sg.residual[t % 4], DMA)

            for t in range(4):
                residual(t)
            for t in range(NT):
                wait_free(sp, ("out", t))
                sp.dma_start(result[bass.ds(b, 1), P * t:P * t + P, :].rearrange("b p c -> p (b c)"),
                             s["tiles"][:, t % 4, :]).then_inc(sg.stored[t % 4], DMA)
                if t + 4 < NT:
                    sp.wait_ge(sg.stored[t % 4], DMA)
                    residual(t + 4)
            for n in range(4):
                sp.wait_ge(sg.stored[n], DMA * (NT // 4))

        @block.gpsimd
        def _(pool):
            if not squared:
                pool.memset(s["k"][STACK:SHIFT, :].bitcast(F32), 1.0).then_inc(sg.built, 1)
                pool.wait_ge(sg.built, 1)
                pool.memset(s["maxima"][:].rearrange("p a i t h -> p (a i t h)"), LOWEST).then_inc(sg.built, 1)
                pool.wait_ge(sg.built, 2)
            pool.wait_ge(sg.variance, 1)
            pool.tensor_tensor(s["rstd"][:], s["var_eps"][:], k["minus_half"][:], ALU.pow).then_inc(sg.rstd, 1)
            pool.wait_ge(sg.rstd, 1)
            if squared:
                for n in range(NG * NSTEPS):
                    c, kb = STEPS[n % NSTEPS]
                    if kb >= TPC * c:
                        off = P * (kb - TPC * c)
                        pool.wait_ge(sg.probs_ready, HG * (n + 1))
                        part = s["probs"][:, n % slots, :, off:off + P]
                        pool.affine_select(out=part, in_=part, compare_op=ALU.is_ge, fill=0.0, base=0,
                                           pattern=[[0, HG], [1, P]], channel_multiplier=-1).then_inc(sg.probs_masked, 1)
            if mqa:
                for t in range(NT):
                    pool.wait_ge(sg.residual[t % 4], DMA * (t // 4 + 1))
                    x = s["tiles"][:, t % 4, :]
                    pool.tensor_tensor(x, x, w["bo"][:], ALU.add).then_inc(sg.biased, 1)

        @block.scalar
        def _(act):
            def high(name, out, source, bias=None):
                wait_work(act, name)
                if bias is None:
                    ins = act.activation(out, source, ACT.Copy)
                else:
                    ins = act.activation(out, source, ACT.Identity, bias=bias)
                ins.then_inc(sg.work_high[bank(name)], 1)

            def pre(g, u):
                name = (u[0], g, *u[1:])
                if u[0] == "q" and not squared:
                    c = u[1]
                    if g:
                        act.wait_ge(sg.stacked[c], DMA * 3 * HG * g)
                    high(name, s["pair"][:, c, HIGH, :], work[:, bank(name), :],
                         w["bq"][:, g:g + 1] if mqa else None)
                if u[0] == "max":
                    high(name, s["shift"][:, g % 2, HIGH, :], work[0:HG * NT, bank(name), 0:P])
                if squared and u[0] in ("q", "k"):
                    n = 4 * g + 2 * (u[0] == "k") + u[1]
                    wait_work(act, name)
                    if n >= 2:
                        act.wait_ge(sg.low_done[n % 2], n // 2)
                    act.activation(s["centred"][:, n % 2, :], work[:, bank(name), :], ACT.Identity,
                                   bias=w["feature_bias"][:, 0:1]).then_inc(sg.centred, 1)
                    if n:
                        wait_work(act, feature_unit(n - 1, "var"))
                    act.activation(s["squares"][:], work[:, bank(name), :], ACT.Square,
                                   bias=w["feature_bias"][:, 0:1]).then_inc(sg.work_free[bank(name)], 1)
                if u[0] in ("qvar", "kvar"):
                    n = 4 * g + 2 * (u[0] == "kvar") + u[1]
                    wait_work(act, name)
                    if n:
                        act.wait_ge(sg.low_done[(n - 1) % 2], (n - 1) // 2 + 1)
                    act.activation(s["deviation"][:], work[:, bank(name), :], ACT.Sqrt, bias=k["eps"][:, 0:1]).then_inc(sg.work_free[bank(name)], 1)

            for t in range(NT):
                name = ("ln", t)
                high(name, s["xnT"][:, HIGH, :, P * t:P * t + P],
                     work[:, bank(name), :].rearrange("p (kc q) -> p kc q", kc=KC))
            if mqa:
                for c in range(NC):
                    name = ("ks", c)
                    high(name, s["k"][0:STACK, CHUNK * c:CHUNK * c + CHUNK], work[0:STACK, bank(name), :], w["bk"][:, 0:1])
            if gated:
                act.wait_ge(sg.gate_shifted, 1)
                act.activation(s["gate_exp"][:], s["logits"][:], ACT.Exp).then_inc(sg.gate_exp, 1)
                for c in range(NC):
                    name = ("kt", c)
                    high(name, s["k"][0:STACK, CHUNK * c:CHUNK * c + CHUNK], work[0:STACK, bank(name), :])
            for _, u in sorted(following.items()):
                pre(0, u)
            for g in range(NG):
                for st, (c, kb) in enumerate(STEPS):
                    n = g * NSTEPS + st
                    off = max(P * (kb - TPC * c), 0)
                    if n >= slots:
                        act.wait_ge(sg.probs_used, n - slots + 1)
                    for i in range(HG):
                        act.wait_ge(sg.scores_ready, HG * n + i + 1)
                        act.activation(s["probs"][:, n % slots, i, off:], psum["scores_t"][:, i % 2, off:],
                                       ACT.Square if squared else ACT.Exp, scale=SCALE).then_inc(sg.probs_ready, 1)
                    if g + 1 < NG and st in following:
                        pre(g + 1, following[st])

        @block.vector
        def _(dve):
            steps = [0]

            def then(ins):
                steps[0] += 1
                ins.then_inc(sg.vector_step, 1)
                dve.wait_ge(sg.vector_step, steps[0])

            def low(name, out, source, high_part, bias=None):
                wait_high(dve, name, highs[name])
                if bias is None:
                    ins = dve.tensor_tensor(out, source, high_part.bitcast(F32), ALU.subtract)
                else:
                    ins = dve.scalar_tensor_tensor(out, source, bias, high_part.bitcast(F32), ALU.add, ALU.subtract)
                return ins.then_inc(sg.work_free[bank(name)], 1)

            dve.wait_ge(sg.loaded, DMA)
            for t in range(NT):
                ins = dve.bn_stats(s["stats"][:, t, :], x_tile(t))
            then(ins)
            for t in range(NT):
                ins = dve.bn_aggr(s["mean_var"][:, t, :], s["stats"][:, t, :])
            then(ins)
            dve.tensor_scalar(s["var_eps"][:], s["mean_var"][:, :, 1], EPS, None, ALU.add).then_inc(sg.variance, 1)
            dve.wait_ge(sg.rstd, 1)

            def normalise(t):
                if t >= 4:
                    wait_work(dve, ("ln", t - 4))
                dve.tensor_scalar(s["tiles"][:, t % 4, :], x_tile(t), s["mean_var"][:, t, 0:1], s["rstd"][:, t:t + 1],
                                  ALU.subtract, ALU.mult).then_inc(sg.normed, 1)

            def split_tile(t):
                name = ("ln", t)
                cols = slice(P * t, P * t + P)
                low(name, s["xnT"][:, LOW, :, cols], work[:, bank(name), :].rearrange("p (kc q) -> p kc q", kc=KC),
                    s["xnT"][:, HIGH, :, cols])

            for t in range(NT + 2):
                if t < NT:
                    normalise(t)
                if t >= 2:
                    split_tile(t - 2)

            def split_keys(name, c, bias):
                cols = slice(CHUNK * c, CHUNK * c + CHUNK)
                part = s["k"][2 * D:STACK, cols]
                return low(name, part, work[2 * D:STACK, bank(name), :], part, bias)

            if mqa:
                for c in range(NC):
                    split_keys(("ks", c), c, w["bk"][2 * D:STACK, 0:1])
                wait_work(dve, ("vs",))
                dve.tensor_tensor(s["v"][:], work[:, bank(("vs",)), 0:NT * D].rearrange("p (t d) -> p t d", t=NT),
                                  w["bv"][:, None, :].broadcast_to([P, NT, D]), ALU.add).then_inc(sg.work_free[bank(("vs",))], 1)
            if gated:
                def each(x):
                    return x[:, :, None].broadcast_to([P, NT, HEADS])

                name = ("gate",)
                wait_work(dve, name)
                gl = work[:, bank(name), 0:NT * HEADS].rearrange("p (t h) -> p t h", t=NT)
                then(dve.reduce_max(s["logit_max"][:], gl, AX_X))
                ins = dve.tensor_tensor(s["logits"][:], gl, each(s["logit_max"]), ALU.subtract)
                ins.then_inc(sg.work_free[bank(name)], 1)
                wait_free(dve, name)
                dve.tensor_single_scalar(s["is_max"][:], s["logits"][:], 0.0, ALU.is_equal).then_inc(sg.gate_shifted, 1)
                dve.wait_ge(sg.gate_shifted, 1)
                then(dve.tensor_tensor(s["is_max"][:], s["is_max"][:], k["rank"][:], ALU.mult))
                then(dve.reduce_max(s["best"][:], s["is_max"][:], AX_X))
                dve.tensor_tensor(s["chosen"][:], k["rank"][:], each(s["best"]), ALU.is_equal)
                dve.wait_ge(sg.gate_exp, 1)
                then(dve.reduce_sum(s["exp_sum"][:], s["gate_exp"][:], AX_X))
                then(dve.reciprocal(s["top"][:], s["exp_sum"][:]))
                then(dve.tensor_tensor(s["gate"][:], s["chosen"][:], each(s["top"]), ALU.mult))
                for t in range(NT):
                    for n, (what, pick) in enumerate((("kall", "chosen"), ("vall", "gate"))):
                        name = (what, t)
                        wait_work(dve, name)
                        ins = dve.tensor_tensor(s["masked"][:, n, :].rearrange("p (h d) -> p h d", h=HEADS),
                                                work[:, bank(name), :].rearrange("p (h d) -> p h d", h=HEADS),
                                                s[pick][:, t, :][:, :, None].broadcast_to([P, HEADS, D]), ALU.mult)
                        ins.then_inc(sg.work_free[bank(name)], 1)
                        wait_free(dve, name)
                        out = s["k_token"][:, t, 0:D] if what == "kall" else s["v"][:, t, :]
                        ins = dve.tensor_reduce(out, s["masked"][:, n, :].rearrange("p (h d) -> p d h", h=HEADS), AX_X, ALU.add)
                        if what == "kall":
                            then(ins)
                            for r in (1, 2):
                                ins = dve.tensor_copy(s["k_token"][:, t, D * r:D * r + D], s["k_token"][:, t, 0:D])
                            ins.then_inc(sg.selected, 1)
                for c in range(NC):
                    split_keys(("kt", c), c, None)

            def pre(g, u):
                name = (u[0], g, *u[1:])
                if squared and u[0] == "v":
                    wait_work(dve, name)
                    dve.tensor_copy(s["v"][:, g % 2, TPC * u[1]:TPC * u[1] + TPC, :],
                                    work[:, bank(name), :].rearrange("p (t d) -> p t d", t=TPC)).then_inc(sg.work_free[bank(name)], 1)
                if not squared and u[0] == "q":
                    c = u[1]
                    low(name, s["pair"][:, c, LOW, :], work[:, bank(name), :], s["pair"][:, c, HIGH, :],
                        w["bq"][:, g:g + 1] if mqa else None)
                if u[0] == "max":
                    dve.wait_ge(sg.piece_used, NPIECES * (g + 1))
                    dve.tensor_reduce(s["minus_max"][:, g % 2, :], s["maxima"][:, g % 2].rearrange("p i t h -> p (i t) h"),
                                      AX_X, ALU.max, negate=True).then_inc(sg.max_ready, 1)
                    low(name, s["shift"][:, g % 2, LOW, :], work[0:HG * NT, bank(name), 0:P], s["shift"][:, g % 2, HIGH, :])
                if u[0] in ("qvar", "kvar"):
                    c = u[1]
                    n = 4 * g + 2 * (u[0] == "kvar") + c
                    m = 2 * g + (u[0] == "kvar")
                    centred, pair = s["centred"][:, n % 2, :], s["pair"][:, c]
                    wait_free(dve, name)
                    dve.wait_ge(sg.centred, n + 1)
                    then(dve.reciprocal(s["inverse"][:], s["deviation"][:]))
                    then(dve.tensor_tensor(centred, centred, s["inverse"][:], ALU.mult))
                    if m:
                        dve.wait_ge(sg.stacked[c], DMA * 3 * HG * m)
                    then(dve.tensor_copy(pair[:, HIGH, :], centred))
                    dve.tensor_tensor(pair[:, LOW, :], centred, pair[:, HIGH, :].bitcast(F32),
                                      ALU.subtract).then_inc(sg.low_done[c], 1)

            def piece(g, j):
                t, i, p = PIECES[j]
                n = g * NPIECES + j
                width = min(P * (t + 1) - CHUNK * p, CHUNK)
                if n == 0:
                    dve.wait_ge(sg.built, 2)
                dve.wait_ge(sg.piece_ready, n + 1)
                dve.reduce_max(s["maxima"][:, g % 2, i, t, p:p + 1], psum["scores"][:, n % 2, 0:width], AX_X).then_inc(sg.piece_used, 1)

            def finish(g, c):
                dve.wait_ge(sg.probs_used, NSTEPS * g + (start(1) if c == 0 else NSTEPS))
                if squared:
                    then(dve.tensor_scalar(s["inverse"][:], psum["sums"][:], EPS, None, ALU.add))
                    then(dve.reciprocal(s["inverse"][:], s["inverse"][:]))
                else:
                    then(dve.reciprocal(s["inverse"][:], psum["sums"][:]))
                dve.tensor_tensor(heads_out(g, c), psum["heads"][:], s["inverse"][:], ALU.mult).then_inc(sg.sums_used, 1)

            for st in range(NSTEPS):
                if st in following:
                    if following[st] == ("max",):
                        for j in range(NPIECES):
                            piece(0, j)
                    pre(0, following[st])
            for g in range(NG):
                for st in range(NSTEPS):
                    if not squared and g + 1 < NG:
                        for j in pieces_at(st, late=False):
                            piece(g + 1, j)
                    if st in (0, start(1)) and g + st:
                        finish(g - (st == 0), 1 if st == 0 else 0)
                    if not squared and g + 1 < NG:
                        for j in pieces_at(st, late=True):
                            piece(g + 1, j)
                    if g + 1 < NG and st in following:
                        pre(g + 1, following[st])
            finish(NG - 1, NC - 1)
            for t in range(NT):
                name = ("out", t)
                x = s["tiles"][:, t % 4, :]
                wait_work(dve, name)
                if mqa:
                    dve.wait_ge(sg.biased, t + 1)
                else:
                    dve.wait_ge(sg.residual[t % 4], DMA * (t // 4 + 1))
                dve.tensor_tensor(x, work[:, bank(name), :], x, ALU.add).then_inc(sg.work_free[bank(name)], 1)

        @block.tensor
        def _(pe):
            def take(name):
                if unit[name] >= 2:
                    pe.wait_ge(sg.work_free[bank(name)], unit[name] // 2)
                return work[:, bank(name), :]

            def ready(name, ins):
                ins.then_inc(sg.work_ready[bank(name)], 1)

            def xn(a, kc, cols):
                return s["xnT"][:, a, kc, cols]

            for t in range(NT):
                pe.wait_ge(sg.normed, t + 1)
                out = take(("ln", t))
                for kc in range(KC):
                    ins = pe.transpose(tile_of(out, kc), tile_of(s["tiles"][:, t % 4, :], kc), k["ident"][:])
                ready(("ln", t), ins)
            for name in (("ln", NT - 2), ("ln", NT - 1)):
                pe.wait_ge(sg.work_free[bank(name)], unit[name] // 2 + 1)

            def token_product(out, t, weight, cols):
                return pair_product(pe, out, lambda a, kc: xn(a, kc, slice(P * t, P * t + P)),
                                    lambda a, kc: w[weight][:, a, kc, cols])

            def channel_product(out, c, weight, cols):
                return pair_product(pe, out, lambda a, kc: w[weight][:, a, kc, cols],
                                    lambda a, kc: xn(a, kc, slice(CHUNK * c, CHUNK * c + CHUNK)))

            if mqa:
                for c in range(NC):
                    out = take(("ks", c))
                    ready(("ks", c), channel_product(out[0:STACK, :], c, "wk", slice(0, STACK)))
                out = take(("vs",))
                for t in range(NT):
                    ins = token_product(out[:, D * t:D * t + D], t, "wv", slice(0, D))
                ready(("vs",), ins)
            if gated:
                out = take(("gate",))
                for t in range(NT):
                    ins = token_product(out[:, HEADS * t:HEADS * t + HEADS], t, "wg", slice(0, HEADS))
                ready(("gate",), ins)
                for t in range(NT):
                    for what, weight in (("kall", "wk"), ("vall", "wv")):
                        ready((what, t), token_product(take((what, t)), t, weight, slice(0, C)))
                for c in range(NC):
                    out = take(("kt", c))
                    for t in range(TPC * c, TPC * c + TPC):
                        pe.wait_ge(sg.selected, t + 1)
                        ins = pe.transpose(tile_of(out, t % TPC)[0:STACK, :], s["k_token"][:, t, :], k["ident"][:])
                    ready(("kt", c), ins)

            def pre(g, u):
                name = (u[0], g, *u[1:])
                cols = slice(P * g, P * g + P)
                if u[0] == "max":
                    pe.wait_ge(sg.max_ready, g + 1)
                    out = take(name)
                    ready(name, pe.transpose(out[0:HG * NT, 0:P], s["minus_max"][:, g % 2, :], k["ident"][:]))
                elif u[0] in ("q", "k"):
                    ready(name, channel_product(take(name), u[1], "w" + u[0], cols))
                elif u[0] == "v":
                    out = take(name)
                    for t in range(TPC):
                        ins = token_product(tile_of(out, t), TPC * u[1] + t, "wv", cols)
                    ready(name, ins)
                else:
                    product = (u[0][0], g, u[1])
                    pe.wait_ge(sg.work_free[bank(product)], unit[product] // 2 + 1)
                    ready(name, pe.matmul(take(name), k["head_mean"][:].rearrange("p i d -> p (i d)"), s["squares"][:],
                                          start=True, stop=True))

            def piece(g, j):
                t, i, p = PIECES[j]
                n = g * NPIECES + j
                width = min(P * (t + 1) - CHUNK * p, CHUNK)
                diagonal = P * (t + 1) <= CHUNK * (p + 1)
                if j == 0:
                    for c in range(NC):
                        pe.wait_ge(sg.stacked[c], DMA * 3 * HG * (g + 1))
                    if g == 0:
                        for c in range(NC):
                            name = ("ks" if mqa else "kt", c)
                            pe.wait_ge(sg.work_free[bank(name)], unit[name] // 2 + 1)
                        pe.wait_ge(sg.built, 2)
                if n >= 2:
                    pe.wait_ge(sg.piece_used, n - 1)
                out = psum["scores"][:, n % 2, :]
                ins = pe.matmul(out[:, 0:width], s["q"][0:STACK, g % 2, i, P * t:P * t + P],
                                s["k"][0:STACK, CHUNK * p:CHUNK * p + width], start=True, stop=not diagonal)
                if diagonal:
                    ins = pe.matmul(out[:, width - P:width], k["ident16"][:], k["mask"][:], start=False, stop=True)
                ins.then_inc(sg.piece_ready, 1)

            def scores(g, st, i):
                c, kb = STEPS[st]
                n = HG * (g * NSTEPS + st) + i
                off = max(P * (kb - TPC * c), 0)
                if n >= 2:
                    pe.wait_ge(sg.probs_ready, n - 1)
                out = psum["scores_t"][:, i % 2, :]
                keys = s["k"][0:rows, g % 2, i, P * kb:P * kb + P] if squared else s["k"][0:rows, P * kb:P * kb + P]
                diagonal = kb >= TPC * c and not squared
                ins = pe.matmul(out[:, off:], keys, s["q"][0:rows, g % 2, i, CHUNK * c + off:CHUNK * c + CHUNK],
                                start=True, stop=not diagonal)
                if diagonal:
                    ins = pe.matmul(out[:, off:off + P], k["ident16"][:], k["mask_t"][:], start=False, stop=True)
                ins.then_inc(sg.scores_ready, 1)

            diagonals = [0]

            def products(n, values):
                g, st = divmod(n, NSTEPS)
                c, kb = STEPS[st]
                off = max(P * (kb - TPC * c), 0)
                last = kb == TPC * (c + 1) - 1
                if values:
                    pe.wait_ge(sg.probs_ready, HG * (n + 1))
                    if squared and kb >= TPC * c:
                        diagonals[0] += 1
                        pe.wait_ge(sg.probs_masked, diagonals[0])
                    if kb == 0 and NC * g + c:
                        pe.wait_ge(sg.sums_used, NC * g + c)
                for i in range(HG):
                    if not values:
                        left, out = k["ones"][:], psum["sums"]
                    elif squared:
                        left, out = s["v"][:, g % 2, kb, D * i:D * i + D], psum["heads"]
                    else:
                        left, out = s["v"][:, kb, :], psum["heads"]
                    ins = pe.matmul(out[D * i:D * i + D, off:], left, s["probs"][:, n % slots, i, off:],
                                    start=(kb == 0), stop=last)
                if not values:
                    ins.then_inc(sg.probs_used, 1)

            for st in range(NSTEPS):
                if st in following:
                    if following[st] == ("max",):
                        for j in range(NPIECES):
                            piece(0, j)
                    pre(0, following[st])
            for g in range(NG):
                if squared:
                    for c in range(NC):
                        pe.wait_ge(sg.stacked[c], DMA * 3 * HG * pairs_made * (g + 1))
                else:
                    pe.wait_ge(sg.shift_moved, DMA * 2 * (g + 1))
                for st in range(NSTEPS):
                    n = g * NSTEPS + st
                    scores(g, st, 0)
                    scores(g, st, 1)
                    if n:
                        products(n - 1, values=True)
                    scores(g, st, 2)
                    if not squared and g + 1 < NG:
                        for j in pieces_at(st, late=False):
                            piece(g + 1, j)
                    scores(g, st, 3)
                    if n:
                        products(n - 1, values=False)
                    if not squared and g + 1 < NG:
                        for j in pieces_at(st, late=True):
                            piece(g + 1, j)
                    if g + 1 < NG and st in following:
                        pre(g + 1, following[st])
            products(NG * NSTEPS - 1, values=True)
            products(NG * NSTEPS - 1, values=False)
            pe.wait_ge(sg.sums_used, NC * NG)
            for t in range(NT):
                name = ("out", t)
                out = take(name)
                for g in range(NG):
                    heads = xy[:, T * g + P * t:T * g + P * t + P]
                    if gated:
                        ins = pe.transpose(tile_of(out, g), heads, k["ident"][:])
                    else:
                        ins = pe.matmul(out, heads, w["wo"][:, g, :], start=(g == 0), stop=(g == NG - 1))
                ready(name, ins)


def build(nc, dram, out):
    with ExitStack() as ctx:
        sg = Signals(nc, ctx)
        psum = {
            "work": ctx.enter_context(nc.psum_tensor("work", [P, 2, CHUNK], F32)),
            "scores": ctx.enter_context(nc.psum_tensor("scores", [P, 2, CHUNK], F32)),
            "scores_t": ctx.enter_context(nc.psum_tensor("scores_t", [P, 2, CHUNK], F32)),
            "heads": ctx.enter_context(nc.psum_tensor("heads", [P, CHUNK], F32)),
            "sums": ctx.enter_context(nc.psum_tensor("sums", [P, CHUNK], F32)),
        }
        k = make_constants(nc, ctx, sg)
        for layer, kind in enumerate(LAYERS):
            with ExitStack() as own:
                def pair(name, n):
                    return own.enter_context(nc.sbuf_tensor(f"{name}_{layer}", [P, 2, KC, n], F32R))

                def plain(name, shape):
                    return own.enter_context(nc.sbuf_tensor(f"{name}_{layer}", shape, F32))

                w = {"wq": pair("wq", C)}
                if kind == "squared":
                    w |= {"wk": pair("wk", C), "wv": pair("wv", C), "wo": plain("wo", [P, KC, C]),
                          "feature_bias": plain("feature_bias", [P, 1])}
                    prepare_squared(nc, sg, k, psum, w, dram["squared"])
                elif kind == "gated":
                    w |= {"wk": pair("wk", C), "wv": pair("wv", C), "wg": pair("wg", HEADS)}
                    prepare_gated(nc, sg, k, psum, w, dram["gated"], layer)
                else:
                    w |= {"wk": pair("wk", STACK), "wv": pair("wv", D), "wo": plain("wo", [P, KC, C]),
                          "bq": plain("bq", [P, NG]), "bk": plain("bk", [STACK, 1]), "bv": plain("bv", [P, D]),
                          "bo": plain("bo", [P, C])}
                    w |= {f"wk{r}": w["wk"][:, :, :, D * r:D * r + D] for r in range(3)}
                    prepare_mqa(nc, sg, k, psum, w, dram["mqa"])
                s = stage_buffers(nc, own, kind, layer)
                with nc.Fori(0, B) as b:
                    stage(nc, sg, k, psum, w, s, kind, b, dram["x"] if layer == 0 else out, out)
                    nc.all_engine_barrier(sems_to_clear=sg.range)


def kernel(**inputs):
    import numpy as np
    import concourse.bacc as bacc
    from concourse.bass_utils import run_bass_kernel_spmd

    def a(name):
        return np.asarray(inputs[f"L0_{name}"])

    arrays = {
        "x": a("attn_a_hidden_states"),
        "squared_wq": a("attn_a_Wq"), "squared_wk": a("attn_a_Wk"), "squared_wvT": a("attn_a_Wv").T,
        "squared_woT": a("attn_a_Wo").T, "squared_gamma": a("attn_a_gamma"), "squared_beta": a("attn_a_beta"),
        "mqa_wqkvT": a("attn_b_Wqkv_w").T, "mqa_bqkv": a("attn_b_Wqkv_b"),
        "mqa_woT": a("attn_b_out_w").T, "mqa_bout": a("attn_b_out_b"),
        "gated_wgateT": a("ffn_W_gate").T, "gated_wqkvT": a("ffn_W_qkv").T,
    }
    arrays = {f"in_{n}": np.ascontiguousarray(v) for n, v in arrays.items()}
    nc = bacc.Bacc("TRN2", target_bir_lowering=False, num_devices=1, dynamic_dma_scratch_size=1024)
    aps = {n: nc.dram_tensor(n, v.shape, F32, kind="ExternalInput").ap() for n, v in arrays.items()}
    dram = {"x": aps["in_x"]}
    for kind in ("squared", "gated", "mqa"):
        start = f"in_{kind}_"
        dram[kind] = {n[len(start):]: ap for n, ap in aps.items() if n.startswith(start)}
    out = nc.dram_tensor("out", (B, T, C), F32, kind="ExternalOutput").ap()
    build(nc, dram, out)
    result = run_bass_kernel_spmd(nc, [arrays], core_ids=[0])
    return result.results[0]["out"]
```

```python
from contextlib import ExitStack

import concourse.bass as bass
from concourse import mybir

F32 = mybir.dt.float32
F32R = mybir.dt.float32r
BF16 = mybir.dt.bfloat16
ALU = mybir.AluOpType
ACT = mybir.ActivationFunctionType
AX_X = mybir.AxisListType.X

P = 128
B, T, C = 4, 1024, 512
HEADS, D = 16, 32
HG = P // D
NG = HEADS // HG
KC = C // P
NT = T // P
CHUNK = 512
NC = T // CHUNK
TPC = CHUNK // P
EPS = 1e-5
SCALE = float(D) ** -0.5
MASKED = -1.0e30
LOWEST = -3.0e38
HIGH, LOW = 0, 1
PAIRS = ((HIGH, HIGH), (HIGH, LOW), (LOW, HIGH))
QUERY_ROWS = (HIGH, LOW, HIGH)
KEY_ROWS = (HIGH, HIGH, LOW)
STACK = 3 * D
SHIFT = STACK + 2
DMA = 16
LAYERS = ("squared", "gated", "mqa", "gated")

STEPS = [(c, kb) for c in range(NC) for kb in range(TPC * (c + 1))]
NSTEPS = len(STEPS)
CHUNK_STEPS = [STEPS.index((c, 0)) for c in range(NC)]
PIECES = [(t, i, p) for t in range(NT) for i in range(HG) for p in range(t // TPC + 1)]
NPIECES = len(PIECES)
PIECES_PER_STEP = 6
PIECE_STEPS = NPIECES // PIECES_PER_STEP
PARTS = 8
PART = CHUNK // PARTS


def layer_norm_events():
    turns = []
    for n in range(NT + 2):
        turn = [("ln", n - 2)] if n >= 2 else []
        turn += [("norm", n - 1)] if 1 <= n <= NT else []
        turn += [("stats", n)] if n < NT else []
        turns.append(turn)
    return turns


def plan(kind, part):
    turns = layer_norm_events()
    features = [("v", 0), ("v", 1), ("q", 0), ("qvar", 0), ("q", 1), ("qvar", 1),
                ("k", 0), ("kvar", 0), ("k", 1), ("kvar", 1)]
    if part == "first":
        events = [e for turn in turns for e in turn]
        if kind == "squared":
            return events + [(u, NG, c) for u, c in features]
        every = [("pieces", NG, PIECES_PER_STEP * n, PIECES_PER_STEP * (n + 1)) for n in range(PIECE_STEPS)]
        if kind == "mqa":
            events += [("ks", 0), ("q", NG, 0), ("ks", 1), ("q", NG, 1), ("vs",)] + every
        else:
            events += [("gate",), ("gate_exp",), ("gate_value",), ("q", NG, 0), ("q", NG, 1)] + [("kall", t) for t in range(NT)]
            events += [("kt", c) for c in range(NC)]
            for t in range(NT):
                events += [every[t], ("vall", t)]
        return events + [("maxred", NG), ("max", NG), ("q", NG + 1, 0)]

    following = part == "middle"
    at = {(g, st): [] for g in range(NG) for st in range(NSTEPS)}
    if kind == "squared":
        for g in range(NG - 1):
            for st, (u, c) in enumerate(features):
                at[g, st].append((u, g + 1, c))
        if following:
            for n, place in enumerate([(2, 5), (2, 6), (2, 7), (2, 8), (2, 9), (2, 10), (2, 11), (2, 11), (3, 0), (3, 0)]):
                at[place] += turns[n]
            for st, (u, c) in zip([1, 1, 2, 3, 4, 5, 6, 7, 8, 9], features):
                at[3, st].append((u, NG, c))
        return at
    for g in range(NG):
        if g + 1 < NG or following:
            at[g, 0].append(("q", g + 1, 1))
            late = 2 if g + 1 == NG else 0
            at[g, PIECE_STEPS + late].append(("maxred", g + 1))
            at[g, PIECE_STEPS + late + 1].append(("max", g + 1))
        if g + 2 < NG or following:
            at[g, 6].append(("q", g + 2, 0))
    if following:
        places = [(1, 4 + n) for n in range(6)] + [(2, n) for n in range(4)]
        for n, place in enumerate(places):
            at[place] += turns[n]
        if kind == "mqa":
            at[2, 5].append(("ks", 0))
            at[2, 7].append(("ks", 1))
            at[2, 8].append(("vs",))
        else:
            at[2, 4].append(("gate",))
            at[2, 5].append(("gate_exp",))
            at[2, 6].append(("gate_value",))
            for t in range(NT):
                at[2, 4 + t].append(("kall", t))
                at[3, 1 + t].append(("vall", t))
            at[2, 9].append(("kt", 0))
            at[3, 0].append(("kt", 1))
    return at


def pieces_at(kind, part, g, st):
    if kind == "squared" or (g + 1 == NG and part != "middle"):
        return []
    n = st - (2 if g + 1 == NG else 0)
    return list(range(PIECES_PER_STEP * n, PIECES_PER_STEP * (n + 1))) if 0 <= n < PIECE_STEPS else []


UNITS = ("ln", "ks", "vs", "gate", "kall", "vall", "kt", "q", "k", "v", "qvar", "kvar", "max", "out")
WITH_HIGH = {"squared": ("ln",), "gated": ("ln", "kt", "q", "max"), "mqa": ("ln", "ks", "q", "max")}


class Count:

    def __init__(self):
        self.n = 0

    def next(self):
        self.n += 1
        return self.n - 1


class Signals:

    def __init__(self, nc, ctx):
        self.all = []

        def sem(name):
            self.all.append(ctx.enter_context(nc.semaphore(name)))
            return self.all[-1]

        self.loaded = sem("loaded")
        self.built = sem("built")
        self.vector_step = sem("vector_step")
        self.scalar_step = sem("scalar_step")
        self.variance = sem("variance")
        self.rstd = sem("rstd")
        self.normed = sem("normed")
        self.tile_in = [sem(f"tile_in{k}") for k in range(4)]
        self.work_ready = [sem(f"work_ready{k}") for k in range(2)]
        self.work_high = [sem(f"work_high{k}") for k in range(2)]
        self.work_free = [sem(f"work_free{k}") for k in range(2)]
        self.gate_shifted = sem("gate_shifted")
        self.gate_exp = sem("gate_exp")
        self.selected = sem("selected")
        self.low_done = [sem(f"low_done{k}") for k in range(2)]
        self.centred = sem("centred")
        self.stacked = [sem(f"stacked{k}") for k in range(2)]
        self.piece_ready = sem("piece_ready")
        self.piece_used = sem("piece_used")
        self.max_ready = sem("max_ready")
        self.shift_moved = sem("shift_moved")
        self.brought = sem("brought")
        self.scores_ready = sem("scores_ready")
        self.probs_ready = sem("probs_ready")
        self.probs_masked = sem("probs_masked")
        self.values_done = sem("values_done")
        self.probs_used = sem("probs_used")
        self.copied = sem("copied")
        self.inverted = sem("inverted")
        self.heads_done = sem("heads_done")
        self.tail_done = sem("tail_done")
        self.biased = sem("biased")
        self.stored = [sem(f"stored{k}") for k in range(4)]
        numbers = [s.num for s in self.all]
        self.range = range(min(numbers), max(numbers) + 1)
        assert len(self.range) == len(self.all)


def make_constants(nc, ctx, sg):
    def sb(name, shape, dt=F32):
        return ctx.enter_context(nc.sbuf_tensor(name, shape, dt))

    k = {
        "ident": sb("ident", [P, P]),
        "ident16": sb("ident16", [P, P], BF16),
        "mask": sb("mask", [P, P], BF16),
        "mask_t": sb("mask_t", [P, P], BF16),
        "ones": sb("ones", [P, D]),
        "head_mean": sb("head_mean", [P, HG, D]),
        "centre": sb("centre", [P, P]),
        "rank": sb("rank", [P, NT, HEADS]),
        "minus_half": sb("minus_half", [P, NT]),
        "eps": sb("eps", [P, 1]),
    }
    with nc.Block() as block:
        @block.gpsimd
        def _(pool):
            pool.memset(k["ident"][:], 0.0).then_inc(sg.built, 1)
            pool.memset(k["ident16"][:], 0.0).then_inc(sg.built, 1)
            pool.memset(k["mask"][:], 0.0).then_inc(sg.built, 1)
            pool.memset(k["mask_t"][:], 0.0).then_inc(sg.built, 1)
            pool.memset(k["ones"][:], 1.0)
            pool.memset(k["head_mean"][:], 1.0 / D).then_inc(sg.built, 1)
            pool.memset(k["minus_half"][:], -0.5)
            pool.memset(k["eps"][:], EPS)
            pool.iota(k["rank"][:], pattern=[[0, NT], [-1, HEADS]], base=HEADS, channel_multiplier=0,
                      allow_small_or_imprecise_dtypes=True)
            pool.wait_ge(sg.built, 5)
            for name in ("ident", "ident16"):
                pool.affine_select(out=k[name][:], in_=k[name][:], compare_op=ALU.not_equal, fill=1.0, base=0,
                                   pattern=[[-1, P]], channel_multiplier=1).then_inc(sg.built, 1)
            pool.affine_select(out=k["mask"][:], in_=k["mask"][:], compare_op=ALU.is_ge, fill=MASKED, base=0,
                               pattern=[[-1, P]], channel_multiplier=1)
            pool.affine_select(out=k["mask_t"][:], in_=k["mask_t"][:], compare_op=ALU.is_ge, fill=MASKED, base=0,
                               pattern=[[1, P]], channel_multiplier=-1)
            pool.affine_select(out=k["head_mean"][:], in_=k["head_mean"][:], compare_op=ALU.is_ge, fill=0.0, base=0,
                               pattern=[[-D, HG], [0, D]], channel_multiplier=1).then_inc(sg.built, 1)
            pool.wait_ge(sg.built, 8)
            pool.affine_select(out=k["head_mean"][:], in_=k["head_mean"][:], compare_op=ALU.is_ge, fill=0.0,
                               base=D - 1, pattern=[[D, HG], [0, D]], channel_multiplier=-1).then_inc(sg.built, 1)
            pool.wait_ge(sg.built, 9)
            pool.tensor_tensor(k["centre"][:], k["ident"][:], k["head_mean"][:].rearrange("p i d -> p (i d)"),
                               ALU.subtract)
    nc.all_engine_barrier(sems_to_clear=sg.range)
    return k


def load_rows(w):
    return w.rearrange("(kc p) n -> p kc n", p=P)


def prepare_squared(nc, sg, k, psum, w, dram):
    with ExitStack() as ctx:
        def sb(name, shape, dt=F32):
            return ctx.enter_context(nc.sbuf_tensor(name, shape, dt))

        raw = {n: sb(f"raw_{n}", [P, NG, C]) for n in ("wq", "wk")}
        raw_v = sb("raw_v", [P, KC, C])
        gamma, beta = sb("gamma", [P, 1]), sb("beta", [P, 1])
        scaled = sb("scaled", [P, P])
        block = ctx.enter_context(nc.Block())

        @block.sync
        def _(sp):
            for n in ("wq", "wk"):
                sp.dma_start(raw[n][:], dram[n].rearrange("(g p) c -> p g c", p=P)).then_inc(sg.loaded, DMA)
            sp.dma_start(raw_v[:], load_rows(dram["wvT"])).then_inc(sg.loaded, DMA)
            sp.dma_start(w["wo"][:], load_rows(dram["woT"])).then_inc(sg.loaded, DMA)
            for i in range(HG):
                sp.dma_start(gamma[D * i:D * i + D, :], dram["gamma"].rearrange("(d a) -> d a", a=1)).then_inc(sg.loaded, DMA)
                sp.dma_start(beta[D * i:D * i + D, :], dram["beta"].rearrange("(d a) -> d a", a=1)).then_inc(sg.loaded, DMA)

        everything = DMA * (4 + 2 * HG)

        @block.vector
        def _(dve):
            dve.wait_ge(sg.loaded, everything)
            dve.tensor_scalar(scaled[:], k["centre"][:], gamma[:, 0:1], None, ALU.mult).then_inc(sg.vector_step, 1)
            dve.wait_ge(sg.scalar_step, 1)
            dve.tensor_tensor(w["wv"][:, LOW], raw_v[:], w["wv"][:, HIGH].bitcast(F32), ALU.subtract)
            for u in range(2 * KC):
                n, kc = ("wq", "wk")[u // KC], u % KC
                dve.wait_ge(sg.scalar_step, 2 + u)
                dve.tensor_tensor(w[n][:, LOW, kc], psum["work"][:, u % 2], w[n][:, HIGH, kc].bitcast(F32),
                                  ALU.subtract).then_inc(sg.work_free[u % 2], 1)
            dve.wait_ge(sg.work_ready[0], KC + 1)
            dve.tensor_copy(w["feature_bias"][:], psum["work"][:, 0, 0:1])

        @block.scalar
        def _(act):
            act.wait_ge(sg.loaded, everything)
            act.activation(w["wv"][:, HIGH], raw_v[:], ACT.Copy).then_inc(sg.scalar_step, 1)
            for u in range(2 * KC):
                n, kc = ("wq", "wk")[u // KC], u % KC
                act.wait_ge(sg.work_ready[u % 2], u // 2 + 1)
                act.activation(w[n][:, HIGH, kc], psum["work"][:, u % 2], ACT.Copy).then_inc(sg.scalar_step, 1)

        @block.tensor
        def _(pe):
            pe.wait_ge(sg.loaded, everything)
            pe.wait_ge(sg.vector_step, 1)
            for u in range(2 * KC):
                n, kc = ("wq", "wk")[u // KC], u % KC
                if u >= 2:
                    pe.wait_ge(sg.work_free[u % 2], u // 2)
                for g in range(NG):
                    mm = pe.matmul(psum["work"][:, u % 2, P * g:P * g + P], raw[n][:, g, P * kc:P * kc + P], scaled[:],
                                   start=True, stop=True)
                mm.then_inc(sg.work_ready[u % 2], 1)
            pe.wait_ge(sg.work_free[0], KC)
            pe.matmul(psum["work"][:, 0, 0:1], k["centre"][:], beta[:], start=True, stop=True).then_inc(sg.work_ready[0], 1)
    nc.all_engine_barrier(sems_to_clear=sg.range)


def prepare_gated(nc, sg, k, psum, w, dram, layer):
    with ExitStack() as ctx:
        n_all = 3 * C
        raw = ctx.enter_context(nc.sbuf_tensor(f"raw_qkv_{layer}", [P, KC, n_all], F32))
        raw_gate = ctx.enter_context(nc.sbuf_tensor(f"raw_gate_{layer}", [P, KC, HEADS], F32))
        block = ctx.enter_context(nc.Block())
        parts = [("wq", raw[:, :, 0:C]), ("wk", raw[:, :, C:2 * C]), ("wv", raw[:, :, 2 * C:3 * C]), ("wg", raw_gate[:])]

        @block.sync
        def _(sp):
            sp.dma_start(raw[:], load_rows(dram["wqkvT"])).then_inc(sg.loaded, DMA)
            sp.dma_start(raw_gate[:], load_rows(dram["wgateT"])).then_inc(sg.loaded, DMA)

        split(block, sg, w, parts, 2 * DMA)
    nc.all_engine_barrier(sems_to_clear=sg.range)


def prepare_mqa(nc, sg, k, psum, w, dram):
    with ExitStack() as ctx:
        n_all = C + 2 * D
        raw = ctx.enter_context(nc.sbuf_tensor("raw_qkv", [P, KC, n_all], F32))
        block = ctx.enter_context(nc.Block())
        parts = [("wq", raw[:, :, 0:C]), ("wv", raw[:, :, C + D:C + 2 * D])]
        parts += [(f"wk{r}", raw[:, :, C:C + D]) for r in range(3)]

        @block.sync
        def _(sp):
            sp.dma_start(raw[:], load_rows(dram["wqkvT"])).then_inc(sg.loaded, DMA)
            sp.dma_start(w["wo"][:], load_rows(dram["woT"])).then_inc(sg.loaded, DMA)
            bias = dram["bqkv"]
            for g in range(NG):
                sp.dma_start(w["bq"][:, g:g + 1], bias[P * g:P * g + P].rearrange("(p a) -> p a", a=1)).then_inc(sg.loaded, DMA)
            for r in range(3):
                sp.dma_start(w["bk"][D * r:D * r + D, :], bias[C:C + D].rearrange("(d a) -> d a", a=1)).then_inc(sg.loaded, DMA)
            sp.dma_start(w["bv"][:], bias[C + D:C + 2 * D].partition_broadcast(P)).then_inc(sg.loaded, DMA)
            sp.dma_start(w["bo"][:], dram["bout"].partition_broadcast(P)).then_inc(sg.loaded, DMA)

        split(block, sg, w, parts, DMA * (7 + NG))
    nc.all_engine_barrier(sems_to_clear=sg.range)


def split(block, sg, w, parts, loads):
    @block.scalar
    def _(act):
        act.wait_ge(sg.loaded, loads)
        for name, raw in parts:
            act.activation(w[name][:, HIGH], raw, ACT.Copy).then_inc(sg.scalar_step, 1)

    @block.vector
    def _(dve):
        for n, (name, raw) in enumerate(parts):
            dve.wait_ge(sg.scalar_step, n + 1)
            dve.tensor_tensor(w[name][:, LOW], raw, w[name][:, HIGH].bitcast(F32), ALU.subtract)


def pair_product(pe, out, left, right):
    terms = [(kc, a, b) for kc in range(KC) for a, b in PAIRS]
    for n, (kc, a, b) in enumerate(terms):
        mm = pe.matmul(out, left(a, kc), right(b, kc), start=(n == 0), stop=(n == len(terms) - 1))
    return mm


def stage_buffers(nc, ctx, kind, layer):
    def sb(name, shape, dt=F32):
        return ctx.enter_context(nc.sbuf_tensor(f"{name}_{layer}", shape, dt))

    s = {
        "y": sb("heads_out", [P, NG, T]),
        "stats": sb("stats", [P, NT, 6]),
        "mean_var": sb("mean_var", [P, NT, 2]),
        "var_eps": sb("var_eps", [P, NT]),
        "rstd": sb("rstd", [P, NT]),
        "tiles": sb("tiles", [P, 4, C]),
        "xnT": sb("xnT", [P, 2, KC, T], F32R),
        "pair": sb("pair", [P, NC, 2, CHUNK], F32R),
        "q": sb("q_stack", [P, 2, HG, T], F32R),
        "sums": sb("sums_out", [P, NC, CHUNK]),
    }
    if kind == "squared":
        s["slots"] = 2
        s["k"] = sb("k_stack", [P, 2, HG, T], F32R)
        s["v"] = sb("v", [P, 2, NT, P])
        s["centred"] = sb("centred_heads", [P, 2, CHUNK])
        s["squares"] = sb("squares", [P, CHUNK])
    else:
        s["slots"] = 3
        s["k"] = sb("k_stack", [P, 2, T], F32R)
        s["v"] = sb("v", [P, 2, NT, D])
        s["maxima"] = sb("maxima", [P, 2, HG, NT, 2])
        s["minus_max"] = sb("minus_max", [P, 2, HG * NT])
        s["shift"] = sb("shift", [HG * NT, 2, 2, P], F32R)
    if kind == "gated":
        for name in ("logits", "gate_exp", "is_max", "chosen", "gate"):
            s[name] = sb(f"g_{name}", [P, NT, HEADS])
        for name in ("logit_max", "exp_sum", "top", "best"):
            s[name] = sb(f"g_{name}", [P, NT])
        s["masked"] = sb("masked_heads", [P, 2, C])
        s["k_token"] = sb("k_token", [P, NT, STACK])
    s["probs"] = sb("probs", [P, s["slots"], HG, CHUNK])
    return s


def stage(nc, sg, k, psum, w, s, kind, part, b, source, result):
    squared, gated, mqa = kind == "squared", kind == "gated", kind == "mqa"
    attends, following = part != "first", part != "last"
    work, slots = psum["work"], s["slots"]
    rows = STACK if squared else SHIFT
    if attends:
        at = plan(kind, part)
        events = [e for place in sorted(at) for e in at[place]] + [("out", t) for t in range(NT)]
    else:
        events = plan(kind, part)

    unit, stack_number, highs = {}, {}, {}
    for name in events:
        if name[0] in UNITS:
            unit[name] = len(unit)
            if name[0] in WITH_HIGH[kind]:
                highs[name] = 1 + sum(unit[h] % 2 == unit[name] % 2 for h in highs)
        if name[0] == ("qvar" if squared else "q") or name[0] == "kvar":
            same = sum(n[2] == name[2] for n in stack_number)
            stack_number[name[0][0], name[1], name[2]] = same
    feature_units = [n for n in events if squared and n[0] in ("q", "k")]
    norm_tiles = [n[1] for n in events if n[0] == "ln"]

    def out_view(t):
        return s["y"][:, :, P * t:P * t + P]

    def tile_of(tensor, t):
        return tensor[:, P * t:P * t + P]

    def bank(name):
        return unit[name] % 2

    def wait_work(eng, name):
        eng.wait_ge(sg.work_ready[bank(name)], unit[name] // 2 + 1)

    def wait_free(eng, name):
        eng.wait_ge(sg.work_free[bank(name)], unit[name] // 2 + 1)

    def wait_high(eng, name):
        eng.wait_ge(sg.work_high[bank(name)], highs[name])

    def wait_stack(eng, name):
        if name in stack_number:
            eng.wait_ge(sg.stacked[name[2]], DMA * 3 * HG * (stack_number[name] + 1))

    def wait_pair_free(eng, name):
        if stack_number[name]:
            eng.wait_ge(sg.stacked[name[2]], DMA * 3 * HG * stack_number[name])

    def keys_of(g):
        return 1 if g >= NG else 0

    with nc.Block() as block:
        @block.sync
        def _(sp):
            def load(t, batch):
                sp.dma_start(s["tiles"][:, t % 4, :],
                             source[bass.ds(batch, 1), P * t:P * t + P, :].rearrange("b p c -> p (b c)"))\
                    .then_inc(sg.tile_in[t % 4], DMA)

            def stack(name, target, parts):
                c = name[2]
                for i in range(HG):
                    for r, half in enumerate(parts):
                        sp.dma_start(target[D * r:D * r + D, name[1] % 2, i, CHUNK * c:CHUNK * c + CHUNK].bitcast(F32),
                                     s["pair"][D * i:D * i + D, c, half, :].bitcast(F32)).then_inc(sg.stacked[c], DMA)

            if norm_tiles:
                for t in range(4):
                    load(t, b + 1)
            for name in events:
                if name[0] == "ln" and name[1] + 4 < NT:
                    wait_work(sp, name)
                    load(name[1] + 4, b + 1)
                if name[0] in ("qvar", "kvar"):
                    stacked = (name[0][0], *name[1:])
                    sp.wait_ge(sg.low_done[name[2]], stack_number[stacked] + 1)
                    stack(stacked, s[name[0][0]], QUERY_ROWS if name[0] == "qvar" else KEY_ROWS)
                if name[0] == "q" and not squared:
                    wait_free(sp, name)
                    stack(name, s["q"], QUERY_ROWS)
                if name[0] == "max":
                    wait_free(sp, name)
                    for half in (HIGH, LOW):
                        sp.dma_start(s["q"][STACK + half:STACK + half + 1, name[1] % 2].rearrange("a i t -> a (i t)").bitcast(F32),
                                     s["shift"][:, name[1] % 2, half, :].bitcast(F32)).then_inc(sg.shift_moved, DMA)
            for c in range(NC):
                stacks = sum(name[2] == c for name in stack_number)
                if stacks:
                    sp.wait_ge(sg.stacked[c], DMA * 3 * HG * stacks)
            shifts = sum(name[0] == "max" for name in events)
            if shifts:
                sp.wait_ge(sg.shift_moved, DMA * 2 * shifts)
            if attends:
                for t in range(4):
                    if norm_tiles:
                        wait_work(sp, ("ln", NT - 4 + t))
                    load(t, b)
                for t in range(NT):
                    wait_free(sp, ("out", t))
                    sp.dma_start(result[bass.ds(b, 1), P * t:P * t + P, :].rearrange("b p c -> p (b c)"),
                                 s["tiles"][:, t % 4, :]).then_inc(sg.stored[t % 4], DMA)
                    if t + 4 < NT:
                        sp.wait_ge(sg.stored[t % 4], DMA)
                        load(t + 4, b)
                for n in range(4):
                    sp.wait_ge(sg.stored[n], DMA * (NT // 4))

        tiles_before = (len(norm_tiles) // 4) * DMA

        @block.gpsimd
        def _(pool):
            if part == "first" and not squared:
                pool.memset(s["k"][STACK:SHIFT, 1, :].bitcast(F32), 1.0).then_inc(sg.built, 1)
                pool.wait_ge(sg.built, 1)
                pool.memset(s["maxima"][:].rearrange("p a i t h -> p (a i t h)"), LOWEST).then_inc(sg.built, 1)
                pool.wait_ge(sg.built, 2)
            variances, diagonals = Count(), Count()

            def roots(names):
                for name in names:
                    if name[0] == "stats":
                        t = name[1]
                        pool.wait_ge(sg.variance, variances.next() + 1)
                        pool.tensor_tensor(s["rstd"][:, t:t + 1], s["var_eps"][:, t:t + 1], k["minus_half"][:, 0:1],
                                           ALU.pow).then_inc(sg.rstd, 1)

            def divide(m):
                g, c = divmod(m, NC)
                pool.wait_ge(sg.copied, 2 * m + 1)
                pool.wait_ge(sg.inverted, PARTS * (m + 1))
                out = s["y"][:, g, CHUNK * c:CHUNK * c + CHUNK]
                pool.tensor_tensor(out, out, s["sums"][:, c, :], ALU.mult).then_inc(sg.heads_done, 1)

            if not attends:
                roots(events)
            else:
                for n in range(NG * NSTEPS):
                    g, st = divmod(n, NSTEPS)
                    c, kb = STEPS[st]
                    if squared and kb >= TPC * c:
                        off = P * (kb - TPC * c)
                        pool.wait_ge(sg.probs_ready, HG * (n + 1))
                        block_part = s["probs"][:, n % slots, :, off:off + P]
                        pool.affine_select(out=block_part, in_=block_part, compare_op=ALU.is_ge, fill=0.0, base=0,
                                           pattern=[[0, HG], [1, P]], channel_multiplier=-1).then_inc(sg.probs_masked, 1)
                    if st == CHUNK_STEPS[1] + 1 and g:
                        divide(NC * g - 1)
                    if st == CHUNK_STEPS[1] + 5:
                        divide(NC * g)
                    roots(at[g, st])
                if mqa:
                    for t in range(NT):
                        pool.wait_ge(sg.tile_in[t % 4], tiles_before + DMA * (t // 4 + 1))
                        x = s["tiles"][:, t % 4, :]
                        pool.tensor_tensor(x, x, w["bo"][:], ALU.add).then_inc(sg.biased, 1)

        @block.scalar
        def _(act):
            features, gates = Count(), Count()

            def high(name, out, source, bias=None):
                wait_work(act, name)
                if bias is None:
                    ins = act.activation(out, source, ACT.Copy)
                else:
                    ins = act.activation(out, source, ACT.Identity, bias=bias)
                ins.then_inc(sg.work_high[bank(name)], 1)

            def take(name):
                u = name[0]
                if u == "ln":
                    t = name[1]
                    high(name, s["xnT"][:, HIGH, :, P * t:P * t + P],
                         work[:, bank(name), :].rearrange("p (kc q) -> p kc q", kc=KC))
                elif u in ("ks", "kt"):
                    c = name[1]
                    high(name, s["k"][0:STACK, 1, CHUNK * c:CHUNK * c + CHUNK], work[0:STACK, bank(name), :],
                         w["bk"][:, 0:1] if mqa else None)
                elif u == "gate_exp":
                    act.wait_ge(sg.gate_shifted, 1)
                    act.activation(s["gate_exp"][:], s["logits"][:], ACT.Exp).then_inc(sg.gate_exp, 1)
                elif u == "q" and not squared:
                    _, g, c = name
                    wait_pair_free(act, name)
                    high(name, s["pair"][:, c, HIGH, :], work[:, bank(name), :],
                         w["bq"][:, g % NG:g % NG + 1] if mqa else None)
                elif u == "max":
                    high(name, s["shift"][:, name[1] % 2, HIGH, :], work[0:HG * NT, bank(name), 0:P])
                elif u in ("q", "k"):
                    n = features.next()
                    wait_work(act, name)
                    if n >= 2:
                        act.wait_ge(sg.low_done[n % 2], n // 2)
                    act.activation(s["centred"][:, n % 2, :], work[:, bank(name), :], ACT.Identity,
                                   bias=w["feature_bias"][:, 0:1]).then_inc(sg.centred, 1)
                    if n:
                        act.wait_ge(sg.low_done[(n - 1) % 2], (n - 1) // 2 + 1)
                    act.activation(s["squares"][:], work[:, bank(name), :], ACT.Square,
                                   bias=w["feature_bias"][:, 0:1]).then_inc(sg.work_free[bank(name)], 1)
                elif u in ("qvar", "kvar"):
                    wait_work(act, name)
                    act.activation(s["squares"][:], work[:, bank(name), :], ACT.Sqrt,
                                   bias=k["eps"][:, 0:1]).then_inc(sg.work_free[bank(name)], 1)

            if not attends:
                for name in events:
                    take(name)
                return

            def probs(n, i):
                g, st = divmod(n, NSTEPS)
                c, kb = STEPS[st]
                off = max(P * (kb - TPC * c), 0)
                act.wait_ge(sg.scores_ready, HG * n + i + 1)
                act.activation(s["probs"][:, n % slots, i, off:], psum["scores_t"][:, i % 2, off:],
                               ACT.Square if squared else ACT.Exp, scale=SCALE).then_inc(sg.probs_ready, 1)

            def copy_heads(m):
                g, c = divmod(m, NC)
                act.wait_ge(sg.values_done, NSTEPS * g + (CHUNK_STEPS[1] if c == 0 else NSTEPS))
                act.activation(s["y"][:, g, CHUNK * c:CHUNK * c + CHUNK], psum["heads"][:], ACT.Copy).then_inc(sg.copied, 1)

            def copy_sums(m):
                g, c = divmod(m, NC)
                act.wait_ge(sg.probs_used, NSTEPS * g + (CHUNK_STEPS[1] if c == 0 else NSTEPS))
                if m >= NC:
                    act.wait_ge(sg.heads_done, m - NC + 1)
                if squared:
                    ins = act.activation(s["sums"][:, c, :], psum["sums"][:], ACT.Identity, bias=k["eps"][:, 0:1])
                else:
                    ins = act.activation(s["sums"][:, c, :], psum["sums"][:], ACT.Copy)
                ins.then_inc(sg.copied, 1)

            for n in range(NG * NSTEPS):
                g, st = divmod(n, NSTEPS)
                whole = [NC * g - 1] if st == 0 and g else [NC * g] if st == CHUNK_STEPS[1] else []
                if n >= slots:
                    act.wait_ge(sg.probs_used, n - slots + 1)
                probs(n, 0)
                for name in at[g, st]:
                    take(name)
                probs(n, 1)
                for m in whole:
                    copy_heads(m)
                probs(n, 2)
                for m in whole:
                    copy_sums(m)
                probs(n, 3)
            copy_heads(NC * NG - 1)
            copy_sums(NC * NG - 1)

        @block.vector
        def _(dve):
            steps, features, pieces, ranked, gates = Count(), Count(), Count(), Count(), Count()

            def then(ins):
                ins.then_inc(sg.vector_step, 1)
                dve.wait_ge(sg.vector_step, steps.next() + 1)

            def low(name, out, source, high_part, bias=None):
                wait_high(dve, name)
                if bias is None:
                    ins = dve.tensor_tensor(out, source, high_part.bitcast(F32), ALU.subtract)
                else:
                    ins = dve.scalar_tensor_tensor(out, source, bias, high_part.bitcast(F32), ALU.add, ALU.subtract)
                ins.then_inc(sg.work_free[bank(name)], 1)

            def each(x):
                return x[:, :, None].broadcast_to([P, NT, HEADS])

            def gate(name):
                wait_work(dve, name)
                gl = work[:, bank(name), 0:NT * HEADS].rearrange("p (t h) -> p t h", t=NT)
                then(dve.reduce_max(s["logit_max"][:], gl, AX_X))
                dve.tensor_tensor(s["logits"][:], gl, each(s["logit_max"]), ALU.subtract)\
                    .then_inc(sg.work_free[bank(name)], 1)
                wait_free(dve, name)
                dve.tensor_single_scalar(s["is_max"][:], s["logits"][:], 0.0, ALU.is_equal).then_inc(sg.gate_shifted, 1)
                dve.wait_ge(sg.gate_shifted, 1)
                then(dve.tensor_tensor(s["is_max"][:], s["is_max"][:], k["rank"][:], ALU.mult))
                then(dve.reduce_max(s["best"][:], s["is_max"][:], AX_X))
                then(dve.tensor_tensor(s["chosen"][:], k["rank"][:], each(s["best"]), ALU.is_equal))

            def gate_value():
                dve.wait_ge(sg.gate_exp, 1)
                then(dve.reduce_sum(s["exp_sum"][:], s["gate_exp"][:], AX_X))
                then(dve.reciprocal(s["top"][:], s["exp_sum"][:]))
                then(dve.tensor_tensor(s["gate"][:], s["chosen"][:], each(s["top"]), ALU.mult))

            def select(name, n, pick, out):
                t = name[1]
                wait_work(dve, name)
                dve.tensor_tensor(s["masked"][:, n, :].rearrange("p (h d) -> p h d", h=HEADS),
                                  work[:, bank(name), :].rearrange("p (h d) -> p h d", h=HEADS),
                                  s[pick][:, t, :][:, :, None].broadcast_to([P, HEADS, D]), ALU.mult)\
                    .then_inc(sg.work_free[bank(name)], 1)
                wait_free(dve, name)
                return dve.tensor_reduce(out, s["masked"][:, n, :].rearrange("p (h d) -> p d h", h=HEADS), AX_X, ALU.add)

            def piece(g, j):
                t, i, p = PIECES[j]
                n = pieces.next()
                width = min(P * (t + 1) - CHUNK * p, CHUNK)
                if n == 0 and part == "first":
                    dve.wait_ge(sg.built, 2)
                dve.wait_ge(sg.piece_ready, n + 1)
                dve.reduce_max(s["maxima"][:, g % 2, i, t, p:p + 1], psum["scores"][:, n % 2, 0:width], AX_X)\
                    .then_inc(sg.piece_used, 1)

            def take(name):
                u = name[0]
                if u == "pieces":
                    for j in range(*name[2:]):
                        piece(name[1], j)
                elif u == "stats":
                    t = name[1]
                    dve.wait_ge(sg.tile_in[t % 4], DMA * (t // 4 + 1))
                    then(dve.bn_stats(s["stats"][:, t, :], s["tiles"][:, t % 4, :]))
                    then(dve.bn_aggr(s["mean_var"][:, t, :], s["stats"][:, t, :]))
                    dve.tensor_scalar(s["var_eps"][:, t:t + 1], s["mean_var"][:, t, 1:2], EPS, None, ALU.add)\
                        .then_inc(sg.variance, 1)
                elif u == "norm":
                    t = name[1]
                    dve.wait_ge(sg.rstd, t + 1)
                    x = s["tiles"][:, t % 4, :]
                    dve.tensor_scalar(x, x, s["mean_var"][:, t, 0:1], s["rstd"][:, t:t + 1], ALU.subtract,
                                      ALU.mult).then_inc(sg.normed, 1)
                elif u == "ln":
                    cols = slice(P * name[1], P * name[1] + P)
                    low(name, s["xnT"][:, LOW, :, cols], work[:, bank(name), :].rearrange("p (kc q) -> p kc q", kc=KC),
                        s["xnT"][:, HIGH, :, cols])
                elif u in ("ks", "kt"):
                    rest = s["k"][2 * D:STACK, 1, CHUNK * name[1]:CHUNK * name[1] + CHUNK]
                    low(name, rest, work[2 * D:STACK, bank(name), :], rest, w["bk"][2 * D:STACK, 0:1] if mqa else None)
                elif u == "vs":
                    wait_work(dve, name)
                    dve.tensor_tensor(s["v"][:, 1], work[:, bank(name), 0:NT * D].rearrange("p (t d) -> p t d", t=NT),
                                      w["bv"][:, None, :].broadcast_to([P, NT, D]), ALU.add)\
                        .then_inc(sg.work_free[bank(name)], 1)
                elif u == "gate":
                    gate(name)
                elif u == "gate_value":
                    gate_value()
                elif u == "kall":
                    t = name[1]
                    then(select(name, 0, "chosen", s["k_token"][:, t, 0:D]))
                    dve.tensor_copy(s["k_token"][:, t, D:STACK].rearrange("p (r d) -> p r d", d=D),
                                    s["k_token"][:, t, 0:D][:, None, :].broadcast_to([P, 2, D])).then_inc(sg.selected, 1)
                elif u == "vall":
                    select(name, 1, "gate", s["v"][:, 1, name[1], :])
                elif u == "v":
                    _, g, half = name
                    wait_work(dve, name)
                    dve.tensor_copy(s["v"][:, g % 2, TPC * half:TPC * half + TPC, :],
                                    work[:, bank(name), :].rearrange("p (t d) -> p t d", t=TPC))\
                        .then_inc(sg.work_free[bank(name)], 1)
                elif u == "q" and not squared:
                    _, g, c = name
                    low(name, s["pair"][:, c, LOW, :], work[:, bank(name), :], s["pair"][:, c, HIGH, :],
                        w["bq"][:, g % NG:g % NG + 1] if mqa else None)
                elif u == "maxred":
                    g = name[1]
                    dve.wait_ge(sg.piece_used, pieces.n)
                    dve.tensor_reduce(s["minus_max"][:, g % 2, :], s["maxima"][:, g % 2].rearrange("p i t h -> p (i t) h"),
                                      AX_X, ALU.max, negate=True).then_inc(sg.max_ready, 1)
                elif u == "max":
                    g = name[1]
                    low(name, s["shift"][:, g % 2, LOW, :], work[0:HG * NT, bank(name), 0:P], s["shift"][:, g % 2, HIGH, :])
                elif u in ("qvar", "kvar"):
                    _, g, c = name
                    n = features.next()
                    stacked = (u[0], g, c)
                    centred, pair = s["centred"][:, n % 2, :], s["pair"][:, c]
                    wait_free(dve, name)
                    dve.wait_ge(sg.centred, n + 1)
                    then(dve.reciprocal(s["squares"][:], s["squares"][:]))
                    then(dve.tensor_tensor(centred, centred, s["squares"][:], ALU.mult))
                    wait_pair_free(dve, stacked)
                    then(dve.tensor_copy(pair[:, HIGH, :], centred))
                    dve.tensor_tensor(pair[:, LOW, :], centred, pair[:, HIGH, :].bitcast(F32),
                                      ALU.subtract).then_inc(sg.low_done[c], 1)

            if not attends:
                for name in events:
                    take(name)
                return

            if not squared:
                dve.tensor_copy(s["k"][0:SHIFT, 0, :], s["k"][0:SHIFT, 1, :].bitcast(F32)).then_inc(sg.brought, 1)
                dve.tensor_copy(s["v"][:, 0], s["v"][:, 1]).then_inc(sg.brought, 1)

            def invert(m, j):
                sums = s["sums"][:, m % NC, PART * j:PART * j + PART]
                dve.wait_ge(sg.copied, 2 * m + 2)
                dve.reciprocal(sums, sums).then_inc(sg.inverted, 1)

            for n in range(NG * NSTEPS):
                g, st = divmod(n, NSTEPS)
                inverses = []
                if g and 1 <= st <= PARTS // 2:
                    inverses = [(NC * g - 1, 2 * (st - 1) + h) for h in range(2)]
                if CHUNK_STEPS[1] < st <= CHUNK_STEPS[1] + PARTS // 2:
                    inverses = [(NC * g, 2 * (st - CHUNK_STEPS[1] - 1) + h) for h in range(2)]
                mine = pieces_at(kind, part, g, st)
                for x in range(3):
                    for j in mine[2 * x:2 * x + 2]:
                        piece(g + 1, j)
                    for m, j in inverses[x:x + 1]:
                        invert(m, j)
                for name in at[g, st]:
                    take(name)

            def add_residual(t):
                name = ("out", t)
                x = s["tiles"][:, t % 4, :]
                wait_work(dve, name)
                if mqa:
                    dve.wait_ge(sg.biased, t + 1)
                else:
                    dve.wait_ge(sg.tile_in[t % 4], tiles_before + DMA * (t // 4 + 1))
                dve.tensor_tensor(x, work[:, bank(name), :], x, ALU.add).then_inc(sg.work_free[bank(name)], 1)

            last = NC * NG - 1
            dve.wait_ge(sg.copied, 2 * last + 2)
            for t in range(TPC):
                sums = s["sums"][:, last % NC, P * t:P * t + P]
                heads = s["y"][:, NG - 1, CHUNK * (NC - 1) + P * t:CHUNK * (NC - 1) + P * t + P]
                then(dve.reciprocal(sums, sums))
                dve.tensor_tensor(heads, heads, sums, ALU.mult).then_inc(sg.tail_done, 1)
                add_residual(t)
            for t in range(TPC, NT):
                add_residual(t)

        @block.tensor
        def _(pe):
            pieces, diagonals, normed = Count(), Count(), Count()
            known = set()

            def free(name):
                if unit[name] >= 2:
                    pe.wait_ge(sg.work_free[bank(name)], unit[name] // 2)
                return work[:, bank(name), :]

            def ready(name, ins):
                ins.then_inc(sg.work_ready[bank(name)], 1)

            def xn(a, kc, cols):
                return s["xnT"][:, a, kc, cols]

            def need_tiles(tiles):
                for t in tiles:
                    if t not in known:
                        known.add(t)
                        wait_free(pe, ("ln", t))

            def token_product(out, t, weight, cols):
                return pair_product(pe, out, lambda a, kc: xn(a, kc, slice(P * t, P * t + P)),
                                    lambda a, kc: w[weight][:, a, kc, cols])

            def channel_product(out, c, weight, cols):
                return pair_product(pe, out, lambda a, kc: w[weight][:, a, kc, cols],
                                    lambda a, kc: xn(a, kc, slice(CHUNK * c, CHUNK * c + CHUNK)))

            def piece(g, j):
                t, i, p = PIECES[j]
                n = pieces.next()
                width = min(P * (t + 1) - CHUNK * p, CHUNK)
                diagonal = P * (t + 1) <= CHUNK * (p + 1)
                if j == 0:
                    wait_stack(pe, ("q", g, 0))
                    if g >= NG:
                        if part == "first":
                            pe.wait_ge(sg.built, 2)
                        for c in range(NC):
                            wait_free(pe, ("ks" if mqa else "kt", c))
                if (t, i, p) == (TPC, 0, 0):
                    wait_stack(pe, ("q", g, 1))
                if n >= 2:
                    pe.wait_ge(sg.piece_used, n - 1)
                out = psum["scores"][:, n % 2, :]
                ins = pe.matmul(out[:, 0:width], s["q"][0:STACK, g % 2, i, P * t:P * t + P],
                                s["k"][0:STACK, keys_of(g), CHUNK * p:CHUNK * p + width], start=True, stop=not diagonal)
                if diagonal:
                    ins = pe.matmul(out[:, width - P:width], k["ident16"][:], k["mask"][:], start=False, stop=True)
                ins.then_inc(sg.piece_ready, 1)

            def take(name):
                u = name[0]
                if u == "pieces":
                    for j in range(*name[2:]):
                        piece(name[1], j)
                elif u == "ln":
                    t = name[1]
                    pe.wait_ge(sg.normed, t + 1)
                    out = free(name)
                    for kc in range(KC):
                        ins = pe.transpose(tile_of(out, kc), tile_of(s["tiles"][:, t % 4, :], kc), k["ident"][:])
                    ready(name, ins)
                elif u == "ks":
                    c = name[1]
                    need_tiles(range(TPC * c, TPC * c + TPC))
                    ready(name, channel_product(free(name)[0:STACK, :], c, "wk", slice(0, STACK)))
                elif u == "vs":
                    need_tiles(range(NT))
                    out = free(name)
                    for t in range(NT):
                        ins = token_product(out[:, D * t:D * t + D], t, "wv", slice(0, D))
                    ready(name, ins)
                elif u == "gate":
                    need_tiles(range(NT))
                    out = free(name)
                    for t in range(NT):
                        ins = token_product(out[:, HEADS * t:HEADS * t + HEADS], t, "wg", slice(0, HEADS))
                    ready(name, ins)
                elif u in ("kall", "vall"):
                    ready(name, token_product(free(name), name[1], "wk" if u == "kall" else "wv", slice(0, C)))
                elif u == "kt":
                    out = free(name)
                    for t in range(TPC):
                        pe.wait_ge(sg.selected, TPC * name[1] + t + 1)
                        ins = pe.transpose(tile_of(out, t)[0:STACK, :], s["k_token"][:, TPC * name[1] + t, :], k["ident"][:])
                    ready(name, ins)
                elif u == "max":
                    pe.wait_ge(sg.max_ready, normed.next() + 1)
                    out = free(name)
                    ready(name, pe.transpose(out[0:HG * NT, 0:P], s["minus_max"][:, name[1] % 2, :], k["ident"][:]))
                elif u in ("q", "k"):
                    _, g, c = name
                    if g >= NG:
                        need_tiles(range(TPC * c, TPC * c + TPC))
                    ready(name, channel_product(free(name), c, "w" + u, slice(P * (g % NG), P * (g % NG) + P)))
                elif u == "v":
                    _, g, half = name
                    if g >= NG:
                        need_tiles(range(TPC * half, TPC * half + TPC))
                    out = free(name)
                    for t in range(TPC):
                        ins = token_product(tile_of(out, t), TPC * half + t, "wv", slice(P * (g % NG), P * (g % NG) + P))
                    ready(name, ins)
                elif u in ("qvar", "kvar"):
                    wait_free(pe, (u[0], *name[1:]))
                    ready(name, pe.matmul(free(name), k["head_mean"][:].rearrange("p i d -> p (i d)"), s["squares"][:],
                                          start=True, stop=True))

            if not attends:
                for name in events:
                    take(name)
                return

            def scores(g, st, i):
                c, kb = STEPS[st]
                n = HG * (g * NSTEPS + st) + i
                off = max(P * (kb - TPC * c), 0)
                if n >= 2:
                    pe.wait_ge(sg.probs_ready, n - 1)
                out = psum["scores_t"][:, i % 2, :]
                keys = s["k"][0:rows, g % 2, i, P * kb:P * kb + P] if squared else s["k"][0:rows, 0, P * kb:P * kb + P]
                diagonal = kb >= TPC * c and not squared
                ins = pe.matmul(out[:, off:], keys, s["q"][0:rows, g % 2, i, CHUNK * c + off:CHUNK * c + CHUNK],
                                start=True, stop=not diagonal)
                if diagonal:
                    ins = pe.matmul(out[:, off:off + P], k["ident16"][:], k["mask_t"][:], start=False, stop=True)
                ins.then_inc(sg.scores_ready, 1)

            def products(n, values):
                g, st = divmod(n, NSTEPS)
                c, kb = STEPS[st]
                off = max(P * (kb - TPC * c), 0)
                if values:
                    if n == 0 and not squared:
                        pe.wait_ge(sg.brought, 2)
                    pe.wait_ge(sg.probs_ready, HG * (n + 1))
                    if squared and kb >= TPC * c:
                        pe.wait_ge(sg.probs_masked, diagonals.next() + 1)
                if kb == 0 and NC * g + c:
                    pe.wait_ge(sg.copied, 2 * (NC * g + c) - values)
                for i in range(HG):
                    if not values:
                        left, out = k["ones"][:], psum["sums"]
                    elif squared:
                        left, out = s["v"][:, g % 2, kb, D * i:D * i + D], psum["heads"]
                    else:
                        left, out = s["v"][:, 0, kb, :], psum["heads"]
                    ins = pe.matmul(out[D * i:D * i + D, off:], left, s["probs"][:, n % slots, i, off:],
                                    start=(kb == 0), stop=(kb == TPC * (c + 1) - 1))
                ins.then_inc(sg.values_done if values else sg.probs_used, 1)

            if not squared:
                pe.wait_ge(sg.brought, 1)
            for g in range(NG):
                for c in range(NC):
                    wait_stack(pe, ("q", g, c))
                    if squared:
                        wait_stack(pe, ("k", g, c))
                if not squared and g:
                    pe.wait_ge(sg.shift_moved, DMA * 2 * g)
                for st in range(NSTEPS):
                    n = g * NSTEPS + st
                    mine = pieces_at(kind, part, g, st)

                    def some(a, z):
                        for j in mine[a:z]:
                            piece(g + 1, j)

                    scores(g, st, 0)
                    some(0, 1)
                    for name in at[g, st]:
                        take(name)
                    scores(g, st, 1)
                    some(1, 2)
                    if n:
                        products(n - 1, values=True)
                    some(2, 3)
                    scores(g, st, 2)
                    some(3, 4)
                    if n:
                        products(n - 1, values=False)
                    some(4, 5)
                    scores(g, st, 3)
                    some(5, 6)
            products(NG * NSTEPS - 1, values=True)
            products(NG * NSTEPS - 1, values=False)
            pe.wait_ge(sg.heads_done, NC * NG - 1)
            for t in range(NT):
                if t >= TPC * (NC - 1):
                    pe.wait_ge(sg.tail_done, t - TPC * (NC - 1) + 1)
                name = ("out", t)
                out = free(name)
                for g in range(NG):
                    if gated:
                        ins = pe.transpose(tile_of(out, g), out_view(t)[:, g, :], k["ident"][:])
                    else:
                        ins = pe.matmul(out, out_view(t)[:, g, :], w["wo"][:, g, :], start=(g == 0), stop=(g == NG - 1))
                ready(name, ins)


def build(nc, dram, out):
    with ExitStack() as ctx:
        sg = Signals(nc, ctx)
        psum = {
            "work": ctx.enter_context(nc.psum_tensor("work", [P, 2, CHUNK], F32)),
            "scores": ctx.enter_context(nc.psum_tensor("scores", [P, 2, CHUNK], F32)),
            "scores_t": ctx.enter_context(nc.psum_tensor("scores_t", [P, 2, CHUNK], F32)),
            "heads": ctx.enter_context(nc.psum_tensor("heads", [P, CHUNK], F32)),
            "sums": ctx.enter_context(nc.psum_tensor("sums", [P, CHUNK], F32)),
        }
        k = make_constants(nc, ctx, sg)
        for layer, kind in enumerate(LAYERS):
            with ExitStack() as own:
                def pair(name, n):
                    return own.enter_context(nc.sbuf_tensor(f"{name}_{layer}", [P, 2, KC, n], F32R))

                def plain(name, shape):
                    return own.enter_context(nc.sbuf_tensor(f"{name}_{layer}", shape, F32))

                w = {"wq": pair("wq", C)}
                if kind == "squared":
                    w |= {"wk": pair("wk", C), "wv": pair("wv", C), "wo": plain("wo", [P, KC, C]),
                          "feature_bias": plain("feature_bias", [P, 1])}
                    prepare_squared(nc, sg, k, psum, w, dram["squared"])
                elif kind == "gated":
                    w |= {"wk": pair("wk", C), "wv": pair("wv", C), "wg": pair("wg", HEADS)}
                    prepare_gated(nc, sg, k, psum, w, dram["gated"], layer)
                else:
                    w |= {"wk": pair("wk", STACK), "wv": pair("wv", D), "wo": plain("wo", [P, KC, C]),
                          "bq": plain("bq", [P, NG]), "bk": plain("bk", [STACK, 1]), "bv": plain("bv", [P, D]),
                          "bo": plain("bo", [P, C])}
                    w |= {f"wk{r}": w["wk"][:, :, :, D * r:D * r + D] for r in range(3)}
                    prepare_mqa(nc, sg, k, psum, w, dram["mqa"])
                s = stage_buffers(nc, own, kind, layer)
                source = dram["x"] if layer == 0 else out
                stage(nc, sg, k, psum, w, s, kind, "first", -1, source, out)
                nc.all_engine_barrier(sems_to_clear=sg.range)
                if B > 1:
                    with nc.Fori(0, B - 1) as b:
                        stage(nc, sg, k, psum, w, s, kind, "middle", b, source, out)
                        nc.all_engine_barrier(sems_to_clear=sg.range)
                stage(nc, sg, k, psum, w, s, kind, "last", B - 1, source, out)
                nc.all_engine_barrier(sems_to_clear=sg.range)


def kernel(**inputs):
    import numpy as np
    import concourse.bacc as bacc
    from concourse.bass_utils import run_bass_kernel_spmd

    def a(name):
        return np.asarray(inputs[f"L0_{name}"])

    arrays = {
        "x": a("attn_a_hidden_states"),
        "squared_wq": a("attn_a_Wq"), "squared_wk": a("attn_a_Wk"), "squared_wvT": a("attn_a_Wv").T,
        "squared_woT": a("attn_a_Wo").T, "squared_gamma": a("attn_a_gamma"), "squared_beta": a("attn_a_beta"),
        "mqa_wqkvT": a("attn_b_Wqkv_w").T, "mqa_bqkv": a("attn_b_Wqkv_b"),
        "mqa_woT": a("attn_b_out_w").T, "mqa_bout": a("attn_b_out_b"),
        "gated_wgateT": a("ffn_W_gate").T, "gated_wqkvT": a("ffn_W_qkv").T,
    }
    arrays = {f"in_{n}": np.ascontiguousarray(v) for n, v in arrays.items()}
    nc = bacc.Bacc("TRN2", target_bir_lowering=False, num_devices=1, dynamic_dma_scratch_size=1024)
    aps = {n: nc.dram_tensor(n, v.shape, F32, kind="ExternalInput").ap() for n, v in arrays.items()}
    dram = {"x": aps["in_x"]}
    for kind in ("squared", "gated", "mqa"):
        start = f"in_{kind}_"
        dram[kind] = {n[len(start):]: ap for n, ap in aps.items() if n.startswith(start)}
    out = nc.dram_tensor("out", (B, T, C), F32, kind="ExternalOutput").ap()
    build(nc, dram, out)
    result = run_bass_kernel_spmd(nc, [arrays], core_ids=[0])
    return result.results[0]["out"]
```

```python
from contextlib import ExitStack

import concourse.bass as bass
from concourse import mybir

F32 = mybir.dt.float32
F32R = mybir.dt.float32r
BF16 = mybir.dt.bfloat16
ALU = mybir.AluOpType
ACT = mybir.ActivationFunctionType
AX_X = mybir.AxisListType.X

P = 128
B, T, C = 4, 1024, 512
HEADS, D = 16, 32
HG = P // D
NG = HEADS // HG
KC = C // P
NT = T // P
CHUNK = 512
NC = T // CHUNK
TPC = CHUNK // P
EPS = 1e-5
SCALE = float(D) ** -0.5
MASKED = -1.0e30
LOWEST = -3.0e38
HIGH, LOW = 0, 1
PAIRS = ((HIGH, HIGH), (HIGH, LOW), (LOW, HIGH))
QUERY_ROWS = (HIGH, LOW, HIGH)
KEY_ROWS = (HIGH, HIGH, LOW)
STACK = 3 * D
SHIFT = STACK + 2
DMA = 16
LAYERS = ("squared", "gated", "mqa", "gated")

STEPS = [(c, kb) for c in range(NC) for kb in range(TPC * (c + 1))]
NSTEPS = len(STEPS)
CHUNK_STEPS = [STEPS.index((c, 0)) for c in range(NC)]


def heads_in_bank(width):
    return CHUNK // width if CHUNK % width == 0 else 1


def offset(st):
    c, kb = STEPS[st]
    return max(P * (kb - TPC * c), 0)


def parts_of(st):
    n = heads_in_bank(CHUNK - offset(st))
    return [(i, n) for i in range(0, HG, n)]


PIECES = []
for _t in range(NT):
    for _p in range(_t // TPC + 1):
        _width = min(P * (_t + 1) - CHUNK * _p, CHUNK)
        _n = heads_in_bank(_width)
        PIECES += [(_t, _p, _width, i, _n) for i in range(0, HG, _n)]
NPIECES = len(PIECES)
SECOND_HALF = next(j for j, piece in enumerate(PIECES) if piece[0] == TPC)
PIECES_PER_STEP = {False: (3, 2, 2, 1, 3, 5, 5, 5, 4, 3, 3, 2), True: (0, 0, 2, 2, 4, 3, 5, 5, 5, 4, 4, 4)}
FIRST_HALF_STEPS = {late: next(n for n in range(NSTEPS) if sum(PIECES_PER_STEP[late][:n]) >= SECOND_HALF) for late in (False, True)}
assert sum(PIECES_PER_STEP[False]) == sum(PIECES_PER_STEP[True]) == NPIECES


SUMS_LATER = 2


def end_of(m):
    g, c = divmod(m, NC)
    return NSTEPS * g + (CHUNK_STEPS[c + 1] if c + 1 < NC else NSTEPS)


def layer_norm_events():
    turns = []
    for n in range(NT + 3):
        turn = [("ln", n - 3)] if n >= 3 else []
        turn += [("norm", n - 2)] if 2 <= n <= NT + 1 else []
        turn += [("stats", n)] if n < NT else []
        turns.append(turn)
    return turns


def plan(kind, part):
    turns = layer_norm_events()
    features = [(("v", 0), ("q", 0)), (("v", 1), ("qvar", 0)), (("qcol", 0), ("q", 1)), (("qwide", 0), ("qvar", 1)),
                (("qrow", 0), ("qcol", 1), ("k", 0)), (("qwide", 1), ("kvar", 0)), (("qrow", 1), ("kcol", 0), ("k", 1)),
                (("kwide", 0), ("kvar", 1)), (("krow", 0), ("kcol", 1)), (("kwide", 1),), (("krow", 1),)]
    if part == "first":
        events = [e for turn in turns for e in turn]
        if kind == "squared":
            return events + [(u, NG, c) for turn in features for u, c in turn]
        every = [("pieces", NG, NPIECES * n // NT, NPIECES * (n + 1) // NT) for n in range(NT)]
        if kind == "mqa":
            events += [("ks", 0), ("q", NG, 0), ("ks", 1), ("q", NG, 1), ("vs",)] + every
        else:
            events += [("gate",), ("gate_exp",), ("gate_value",), ("q", NG, 0), ("q", NG, 1)] + [("kall", t) for t in range(NT)]
            events += [("kt", c) for c in range(NC)]
            for t in range(NT):
                events += [every[t], ("vall", t)]
        return events + [("maxred", NG, 0), ("max", NG, 0), ("q", NG + 1, 0)]

    following = part == "middle"
    at = {(g, st): [] for g in range(NG) for st in range(NSTEPS)}
    for m in range(NC * NG - 1):
        for n, u in enumerate(("sums", "sumcol", "sumwide", "sumrow")):
            at[divmod(end_of(m) + (0 if kind == "squared" else SUMS_LATER) + n, NSTEPS)].append((u, m))
    if kind == "squared":
        for g in range(NG - 1):
            for st, turn in enumerate(features):
                at[g, st] += [(u, g + 1, c) for u, c in turn]
        if following:
            for n, turn in enumerate(turns):
                at[divmod(2 * NSTEPS + 4 + n, NSTEPS)] += turn
            for st, turn in enumerate(features):
                at[3, st + 1] += [(u, NG, c) for u, c in turn]
        return at
    for g in range(NG):
        at[g, 0].append(("maxred", g, 1))
        at[g, 1].append(("max", g, 1))
        if g + 1 < NG or following:
            at[g, 1].append(("q", g + 1, 1))
            half = FIRST_HALF_STEPS[g + 1 == NG]
            at[g, half].append(("maxred", g + 1, 0))
            at[g, half + 1].append(("max", g + 1, 0))
        if g + 2 < NG or following:
            at[g, 6].append(("q", g + 2, 0))
    if following:
        places = [(1, 3 + n) for n in range(7)] + [(2, 1 + n) for n in range(4)]
        for n, place in enumerate(places):
            at[place] += turns[n]
        if kind == "mqa":
            at[2, 5].append(("ks", 0))
            at[2, 7].append(("ks", 1))
            at[2, 8].append(("vs",))
        else:
            at[2, 5].append(("gate",))
            at[2, 6].append(("gate_exp",))
            at[2, 7].append(("gate_value",))
            for t in range(NT):
                at[divmod(2 * NSTEPS + 5 + t, NSTEPS)].append(("kall", t))
                at[3, 2 + t].append(("vall", t))
            at[2, 10].append(("kt", 0))
            at[3, 1].append(("kt", 1))
    return at


def pieces_at(kind, part, g, st):
    if kind == "squared" or (g + 1 == NG and part != "middle"):
        return []
    counts = PIECES_PER_STEP[g + 1 == NG]
    return list(range(sum(counts[:st]), sum(counts[:st + 1])))


UNITS = ("ln", "ks", "vs", "gate", "kall", "vall", "kt", "q", "k", "v", "qvar", "kvar", "qcol", "kcol", "qrow", "krow",
         "sums", "sumcol", "sumrow", "max", "out")
WITH_HIGH = {"squared": ("ln",), "gated": ("ln", "kt", "q", "max"), "mqa": ("ln", "ks", "q", "max")}


class Count:

    def __init__(self):
        self.n = 0

    def next(self):
        self.n += 1
        return self.n - 1


class Signals:

    def __init__(self, nc, ctx):
        self.all = []

        def sem(name):
            self.all.append(ctx.enter_context(nc.semaphore(name)))
            return self.all[-1]

        self.loaded = sem("loaded")
        self.built = sem("built")
        self.vector_step = sem("vector_step")
        self.scalar_step = sem("scalar_step")
        self.variance = sem("variance")
        self.rstd = sem("rstd")
        self.normed = sem("normed")
        self.tile_in = [sem(f"tile_in{k}") for k in range(4)]
        self.work_ready = [sem(f"work_ready{k}") for k in range(2)]
        self.work_high = [sem(f"work_high{k}") for k in range(2)]
        self.work_free = [sem(f"work_free{k}") for k in range(2)]
        self.gate_shifted = sem("gate_shifted")
        self.gate_exp = sem("gate_exp")
        self.selected = sem("selected")
        self.low_done = [sem(f"low_done{k}") for k in range(2)]
        self.centred = sem("centred")
        self.stacked = [sem(f"stacked{k}") for k in range(2)]
        self.piece_ready = sem("piece_ready")
        self.piece_used = sem("piece_used")
        self.max_ready = sem("max_ready")
        self.shift_moved = [sem(f"shift_moved{k}") for k in range(2)]
        self.brought = sem("brought")
        self.scores_ready = sem("scores_ready")
        self.probs_ready = sem("probs_ready")
        self.probs_masked = sem("probs_masked")
        self.values_done = sem("values_done")
        self.summed = sem("summed")
        self.added = sem("added")
        self.heads_copied = sem("heads_copied")
        self.widened = sem("widened")
        self.sums_copied = sem("sums_copied")
        self.biased = sem("biased")
        self.stored = [sem(f"stored{k}") for k in range(4)]
        numbers = [s.num for s in self.all]
        self.range = range(min(numbers), max(numbers) + 1)
        assert len(self.range) == len(self.all)


def make_constants(nc, ctx, sg):
    def sb(name, shape, dt=F32):
        return ctx.enter_context(nc.sbuf_tensor(name, shape, dt))

    k = {
        "ident": sb("ident", [P, P]),
        "ident16": sb("ident16", [P, P], BF16),
        "mask": sb("mask", [P, P], BF16),
        "mask_t": sb("mask_t", [P, P], BF16),
        "ones": sb("ones", [P, D]),
        "head_mean": sb("head_mean", [P, HG, D]),
        "centre": sb("centre", [P, P]),
        "rank": sb("rank", [P, NT, HEADS]),
        "minus_half": sb("minus_half", [P, NT]),
        "eps": sb("eps", [P, 1]),
    }
    with nc.Block() as block:
        @block.gpsimd
        def _(pool):
            pool.memset(k["ident"][:], 0.0).then_inc(sg.built, 1)
            pool.memset(k["ident16"][:], 0.0).then_inc(sg.built, 1)
            pool.memset(k["mask"][:], 0.0).then_inc(sg.built, 1)
            pool.memset(k["mask_t"][:], 0.0).then_inc(sg.built, 1)
            pool.memset(k["ones"][:], 1.0)
            pool.memset(k["head_mean"][:], 1.0 / D).then_inc(sg.built, 1)
            pool.memset(k["minus_half"][:], -0.5)
            pool.memset(k["eps"][:], EPS)
            pool.iota(k["rank"][:], pattern=[[0, NT], [-1, HEADS]], base=HEADS, channel_multiplier=0,
                      allow_small_or_imprecise_dtypes=True)
            pool.wait_ge(sg.built, 5)
            for name in ("ident", "ident16"):
                pool.affine_select(out=k[name][:], in_=k[name][:], compare_op=ALU.not_equal, fill=1.0, base=0,
                                   pattern=[[-1, P]], channel_multiplier=1).then_inc(sg.built, 1)
            pool.affine_select(out=k["mask"][:], in_=k["mask"][:], compare_op=ALU.is_ge, fill=MASKED, base=0,
                               pattern=[[-1, P]], channel_multiplier=1)
            pool.affine_select(out=k["mask_t"][:], in_=k["mask_t"][:], compare_op=ALU.is_ge, fill=MASKED, base=0,
                               pattern=[[1, P]], channel_multiplier=-1)
            pool.affine_select(out=k["head_mean"][:], in_=k["head_mean"][:], compare_op=ALU.is_ge, fill=0.0, base=0,
                               pattern=[[-D, HG], [0, D]], channel_multiplier=1).then_inc(sg.built, 1)
            pool.wait_ge(sg.built, 8)
            pool.affine_select(out=k["head_mean"][:], in_=k["head_mean"][:], compare_op=ALU.is_ge, fill=0.0,
                               base=D - 1, pattern=[[D, HG], [0, D]], channel_multiplier=-1).then_inc(sg.built, 1)
            pool.wait_ge(sg.built, 9)
            pool.tensor_tensor(k["centre"][:], k["ident"][:], k["head_mean"][:].rearrange("p i d -> p (i d)"),
                               ALU.subtract)
    nc.all_engine_barrier(sems_to_clear=sg.range)
    return k


def load_rows(w):
    return w.rearrange("(kc p) n -> p kc n", p=P)


def prepare_squared(nc, sg, k, psum, w, dram):
    with ExitStack() as ctx:
        def sb(name, shape, dt=F32):
            return ctx.enter_context(nc.sbuf_tensor(name, shape, dt))

        raw = {n: sb(f"raw_{n}", [P, NG, C]) for n in ("wq", "wk")}
        raw_v = sb("raw_v", [P, KC, C])
        gamma, beta = sb("gamma", [P, 1]), sb("beta", [P, 1])
        scaled = sb("scaled", [P, P])
        block = ctx.enter_context(nc.Block())

        @block.sync
        def _(sp):
            for n in ("wq", "wk"):
                sp.dma_start(raw[n][:], dram[n].rearrange("(g p) c -> p g c", p=P)).then_inc(sg.loaded, DMA)
            sp.dma_start(raw_v[:], load_rows(dram["wvT"])).then_inc(sg.loaded, DMA)
            sp.dma_start(w["wo"][:], load_rows(dram["woT"])).then_inc(sg.loaded, DMA)
            for i in range(HG):
                sp.dma_start(gamma[D * i:D * i + D, :], dram["gamma"].rearrange("(d a) -> d a", a=1)).then_inc(sg.loaded, DMA)
                sp.dma_start(beta[D * i:D * i + D, :], dram["beta"].rearrange("(d a) -> d a", a=1)).then_inc(sg.loaded, DMA)

        everything = DMA * (4 + 2 * HG)

        @block.vector
        def _(dve):
            dve.wait_ge(sg.loaded, everything)
            dve.tensor_scalar(scaled[:], k["centre"][:], gamma[:, 0:1], None, ALU.mult).then_inc(sg.vector_step, 1)
            dve.wait_ge(sg.scalar_step, 1)
            dve.tensor_tensor(w["wv"][:, LOW], raw_v[:], w["wv"][:, HIGH].bitcast(F32), ALU.subtract)
            for u in range(2 * KC):
                n, kc = ("wq", "wk")[u // KC], u % KC
                dve.wait_ge(sg.scalar_step, 2 + u)
                dve.tensor_tensor(w[n][:, LOW, kc], psum[:, u % 2], w[n][:, HIGH, kc].bitcast(F32),
                                  ALU.subtract).then_inc(sg.work_free[u % 2], 1)
            dve.wait_ge(sg.work_ready[0], KC + 1)
            dve.tensor_copy(w["feature_bias"][:], psum[:, 0, 0:1])

        @block.scalar
        def _(act):
            act.wait_ge(sg.loaded, everything)
            act.activation(w["wv"][:, HIGH], raw_v[:], ACT.Copy).then_inc(sg.scalar_step, 1)
            for u in range(2 * KC):
                n, kc = ("wq", "wk")[u // KC], u % KC
                act.wait_ge(sg.work_ready[u % 2], u // 2 + 1)
                act.activation(w[n][:, HIGH, kc], psum[:, u % 2], ACT.Copy).then_inc(sg.scalar_step, 1)

        @block.tensor
        def _(pe):
            pe.wait_ge(sg.loaded, everything)
            pe.wait_ge(sg.vector_step, 1)
            for u in range(2 * KC):
                n, kc = ("wq", "wk")[u // KC], u % KC
                if u >= 2:
                    pe.wait_ge(sg.work_free[u % 2], u // 2)
                for g in range(NG):
                    mm = pe.matmul(psum[:, u % 2, P * g:P * g + P], raw[n][:, g, P * kc:P * kc + P], scaled[:],
                                   start=True, stop=True)
                mm.then_inc(sg.work_ready[u % 2], 1)
            pe.wait_ge(sg.work_free[0], KC)
            pe.matmul(psum[:, 0, 0:1], k["centre"][:], beta[:], start=True, stop=True).then_inc(sg.work_ready[0], 1)
    nc.all_engine_barrier(sems_to_clear=sg.range)


def prepare_gated(nc, sg, k, psum, w, dram, layer):
    with ExitStack() as ctx:
        n_all = 3 * C
        raw = ctx.enter_context(nc.sbuf_tensor(f"raw_qkv_{layer}", [P, KC, n_all], F32))
        raw_gate = ctx.enter_context(nc.sbuf_tensor(f"raw_gate_{layer}", [P, KC, HEADS], F32))
        block = ctx.enter_context(nc.Block())
        parts = [("wq", raw[:, :, 0:C]), ("wk", raw[:, :, C:2 * C]), ("wv", raw[:, :, 2 * C:3 * C]), ("wg", raw_gate[:])]

        @block.sync
        def _(sp):
            sp.dma_start(raw[:], load_rows(dram["wqkvT"])).then_inc(sg.loaded, DMA)
            sp.dma_start(raw_gate[:], load_rows(dram["wgateT"])).then_inc(sg.loaded, DMA)

        split(block, sg, w, parts, 2 * DMA)
    nc.all_engine_barrier(sems_to_clear=sg.range)


def prepare_mqa(nc, sg, k, psum, w, dram):
    with ExitStack() as ctx:
        n_all = C + 2 * D
        raw = ctx.enter_context(nc.sbuf_tensor("raw_qkv", [P, KC, n_all], F32))
        block = ctx.enter_context(nc.Block())
        parts = [("wq", raw[:, :, 0:C]), ("wv", raw[:, :, C + D:C + 2 * D])]
        parts += [(f"wk{r}", raw[:, :, C:C + D]) for r in range(3)]

        @block.sync
        def _(sp):
            sp.dma_start(raw[:], load_rows(dram["wqkvT"])).then_inc(sg.loaded, DMA)
            sp.dma_start(w["wo"][:], load_rows(dram["woT"])).then_inc(sg.loaded, DMA)
            bias = dram["bqkv"]
            for g in range(NG):
                sp.dma_start(w["bq"][:, g:g + 1], bias[P * g:P * g + P].rearrange("(p a) -> p a", a=1)).then_inc(sg.loaded, DMA)
            for r in range(3):
                sp.dma_start(w["bk"][D * r:D * r + D, :], bias[C:C + D].rearrange("(d a) -> d a", a=1)).then_inc(sg.loaded, DMA)
            sp.dma_start(w["bv"][:], bias[C + D:C + 2 * D].partition_broadcast(P)).then_inc(sg.loaded, DMA)
            sp.dma_start(w["bo"][:], dram["bout"].partition_broadcast(P)).then_inc(sg.loaded, DMA)

        split(block, sg, w, parts, DMA * (7 + NG))
    nc.all_engine_barrier(sems_to_clear=sg.range)


def split(block, sg, w, parts, loads):
    @block.scalar
    def _(act):
        act.wait_ge(sg.loaded, loads)
        for name, raw in parts:
            act.activation(w[name][:, HIGH], raw, ACT.Copy).then_inc(sg.scalar_step, 1)

    @block.vector
    def _(dve):
        for n, (name, raw) in enumerate(parts):
            dve.wait_ge(sg.scalar_step, n + 1)
            dve.tensor_tensor(w[name][:, LOW], raw, w[name][:, HIGH].bitcast(F32), ALU.subtract)


def pair_product(pe, out, left, right):
    terms = [(kc, a, b) for kc in range(KC) for a, b in PAIRS]
    for n, (kc, a, b) in enumerate(terms):
        mm = pe.matmul(out, left(a, kc), right(b, kc), start=(n == 0), stop=(n == len(terms) - 1))
    return mm


def stage_buffers(nc, ctx, kind, layer):
    def sb(name, shape, dt=F32):
        return ctx.enter_context(nc.sbuf_tensor(f"{name}_{layer}", shape, dt))

    s = {
        "y": sb("heads_out", [P, NG, T]),
        "stats": sb("stats", [P, NT, 6]),
        "mean_var": sb("mean_var", [P, NT, 2]),
        "var_eps": sb("var_eps", [P, NT]),
        "rstd": sb("rstd", [P, NT]),
        "tiles": sb("tiles", [P, 4, C]),
        "xnT": sb("xnT", [P, 2, KC, T], F32R),
        "pair": sb("pair", [P, NC, 2, CHUNK], F32R),
        "q": sb("q_stack", [P, 2, NC, HG, CHUNK], F32R),
        "sums": sb("sums_out", [P, CHUNK]),
        "inverse": sb("inverse", [P, TPC, HG]),
        "wide_inverse": sb("wide_inverse", [P, CHUNK]),
    }
    if kind == "squared":
        s["slots"] = 2
        s["k"] = sb("k_stack", [P, 2, HG, T], F32R)
        s["v"] = sb("v", [P, 2, NT, P])
        s["centred"] = sb("centred_heads", [P, 2, CHUNK])
        s["squares"] = sb("squares", [P, CHUNK])
    else:
        s["slots"] = 3
        s["k"] = sb("k_stack", [P, 2, T], F32R)
        s["v"] = sb("v", [P, 2, NT, D])
        s["maxima"] = sb("maxima", [P, 2, HG, NT, 2])
        s["minus_max"] = sb("minus_max", [P, NC, HG * TPC])
        s["shift"] = sb("shift", [HG * TPC, NC, 2, P], F32R)
        s["first_probs"] = sb("first_probs", [P, 2, HG, CHUNK])
    if kind == "gated":
        for name in ("logits", "gate_exp", "is_max", "chosen", "gate"):
            s[name] = sb(f"g_{name}", [P, NT, HEADS])
        for name in ("logit_max", "exp_sum", "top", "best"):
            s[name] = sb(f"g_{name}", [P, NT])
        s["masked"] = sb("masked_heads", [P, 2, C])
        s["k_token"] = sb("k_token", [P, NT, STACK])
    s["probs"] = sb("probs", [P, s["slots"], HG, CHUNK])
    return s


def stage(nc, sg, k, psum, w, s, kind, part, b, source, result):
    squared, gated, mqa = kind == "squared", kind == "gated", kind == "mqa"
    attends, following = part != "first", part != "last"
    work, heads = psum[:, 0:2], psum[:, 2]
    piece_banks, score_banks = psum[:, 3:5], psum[:, 4:8] if squared else psum[:, 5:8]
    sums_bank = psum[:, 3]
    nbanks = 4 if squared else 3
    slots = s["slots"]
    rows = STACK if squared else SHIFT
    if attends:
        at = plan(kind, part)
        events = [e for place in sorted(at) for e in at[place]]
        tail = [("sums", NC * NG - 1), ("sumcol", NC * NG - 1), ("sumwide", NC * NG - 1), ("sumrow", NC * NG - 1)] + [("out", t) for t in range(NT)]
        events += tail
    else:
        events = plan(kind, part)

    unit, stack_number, highs = {}, {}, {}
    for name in events:
        if name[0] in UNITS and not (squared and name[0] == "sums"):
            unit[name] = len(unit)
            if name[0] in WITH_HIGH[kind]:
                highs[name] = 1 + sum(unit[h] % 2 == unit[name] % 2 for h in highs)
        if name[0] == ("qrow" if squared else "q") or name[0] == "krow":
            same = sum(n[2] == name[2] for n in stack_number)
            stack_number[name[0][0], name[1], name[2]] = same
    feature_units = [n for n in events if squared and n[0] in ("q", "k")]
    wide_events = [n for n in events if n[0].endswith("wide")]
    norm_tiles = [n[1] for n in events if n[0] == "ln"]

    def out_view(t):
        return s["y"][:, :, P * t:P * t + P]

    def tile_of(tensor, t):
        return tensor[:, P * t:P * t + P]

    def bank(name):
        return unit[name] % 2

    def wait_work(eng, name):
        eng.wait_ge(sg.work_ready[bank(name)], unit[name] // 2 + 1)

    def wait_free(eng, name):
        eng.wait_ge(sg.work_free[bank(name)], unit[name] // 2 + 1)

    def wait_high(eng, name):
        eng.wait_ge(sg.work_high[bank(name)], highs[name])

    def wait_stack(eng, name):
        if name in stack_number:
            eng.wait_ge(sg.stacked[name[2]], DMA * 3 * HG * (stack_number[name] + 1))

    def wait_pair_free(eng, name):
        if stack_number[name]:
            eng.wait_ge(sg.stacked[name[2]], DMA * 3 * HG * stack_number[name])

    def ring(n):
        g, st = divmod(n, NSTEPS)
        return n if squared else n - NC * g - (1 if st < CHUNK_STEPS[1] else NC)

    def probs_of(n):
        g, st = divmod(n, NSTEPS)
        c, kb = STEPS[st]
        if kb == 0 and not squared:
            return s["first_probs"][:, c]
        return s["probs"][:, ring(n) % slots]

    scores_before = [sum(len(parts_of(st)) for st in range(n % NSTEPS)) + n // NSTEPS * sum(map(len, map(parts_of, range(NSTEPS))))
                     for n in range(NG * NSTEPS + 1)]

    def keys_of(g):
        return 1 if g >= NG else 0

    def load(eng, t, batch):
        eng.dma_start(s["tiles"][:, t % 4, :],
                      source[bass.ds(batch, 1), P * t:P * t + P, :].rearrange("b p c -> p (b c)"))\
            .then_inc(sg.tile_in[t % 4], DMA)

    with nc.Block() as block:
        @block.sync
        def _(sp):
            def stack(name, parts):
                u, g, c = name
                for i in range(HG):
                    for r, half in enumerate(parts):
                        into = s["q"][D * r:D * r + D, g % 2, c, i, :] if u == "q" else \
                            s["k"][D * r:D * r + D, g % 2, i, CHUNK * c:CHUNK * c + CHUNK]
                        sp.dma_start(into.bitcast(F32), s["pair"][D * i:D * i + D, c, half, :].bitcast(F32))\
                            .then_inc(sg.stacked[c], DMA)

            if norm_tiles:
                for t in range(4):
                    load(sp, t, b + 1)
            for name in events:
                if name[0] in ("qrow", "krow"):
                    stacked = (name[0][0], *name[1:])
                    sp.wait_ge(sg.low_done[name[2]], stack_number[stacked] + 1)
                    stack(stacked, QUERY_ROWS if name[0] == "qrow" else KEY_ROWS)
                if name[0] == "q" and not squared:
                    wait_free(sp, name)
                    stack(name, QUERY_ROWS)
                if name[0] == "max":
                    wait_free(sp, name)
                    for half in (HIGH, LOW):
                        sp.dma_start(s["q"][STACK + half:STACK + half + 1, name[1] % 2, name[2]]
                                     .rearrange("a i t -> a (i t)").bitcast(F32),
                                     s["shift"][:, name[2], half, :].bitcast(F32)).then_inc(sg.shift_moved[name[2]], DMA)
            for c in range(NC):
                stacks = sum(name[2] == c for name in stack_number)
                if stacks:
                    sp.wait_ge(sg.stacked[c], DMA * 3 * HG * stacks)
                shifts = sum(name[0] == "max" and name[2] == c for name in events)
                if shifts:
                    sp.wait_ge(sg.shift_moved[c], DMA * 2 * shifts)
            if attends:
                for t in range(4):
                    if norm_tiles:
                        wait_work(sp, ("ln", NT - 4 + t))
                    load(sp, t, b)
                for t in range(NT):
                    wait_free(sp, ("out", t))
                    sp.dma_start(result[bass.ds(b, 1), P * t:P * t + P, :].rearrange("b p c -> p (b c)"),
                                 s["tiles"][:, t % 4, :]).then_inc(sg.stored[t % 4], DMA)
                    if t + 4 < NT:
                        sp.wait_ge(sg.stored[t % 4], DMA)
                        load(sp, t + 4, b)
                for n in range(4):
                    sp.wait_ge(sg.stored[n], DMA * (NT // 4))

        tiles_before = (len(norm_tiles) // 4) * DMA

        @block.gpsimd
        def _(pool):
            if part == "first" and not squared:
                pool.memset(s["k"][STACK:SHIFT, 1, :].bitcast(F32), 1.0).then_inc(sg.built, 1)
                pool.wait_ge(sg.built, 1)
                pool.memset(s["maxima"][:].rearrange("p a i t h -> p (a i t h)"), LOWEST).then_inc(sg.built, 1)
                pool.wait_ge(sg.built, 2)
            variances, diagonals = Count(), Count()

            def roots(names):
                for name in names:
                    if name[0] == "stats":
                        t = name[1]
                        pool.wait_ge(sg.variance, variances.next() + 1)
                        pool.tensor_tensor(s["rstd"][:, t:t + 1], s["var_eps"][:, t:t + 1], k["minus_half"][:, 0:1],
                                           ALU.pow).then_inc(sg.rstd, 1)

            def add(n, half):
                g, st = divmod(n, NSTEPS)
                c, kb = STEPS[st]
                if kb == 0:
                    return
                pool.wait_ge(sg.probs_ready, scores_before[n + 1])
                pool.wait_ge(sg.values_done, n - kb + 1)
                if ring(n):
                    pool.wait_ge(sg.added, 2 * ring(n) - 1 + half)
                some = slice(HG // 2 * half, HG // 2 * half + HG // 2)
                total = s["first_probs"][:, c, some, offset(st):]
                pool.tensor_tensor(total, total, probs_of(n)[:, some, offset(st):], ALU.add).then_inc(sg.added, 1)

            if not attends:
                roots(events)
            else:
                for n in range(NG * NSTEPS):
                    g, st = divmod(n, NSTEPS)
                    c, kb = STEPS[st]
                    if squared and kb >= TPC * c:
                        off = P * (kb - TPC * c)
                        pool.wait_ge(sg.probs_ready, scores_before[n + 1])
                        block_part = probs_of(n)[:, :, off:off + P]
                        pool.affine_select(out=block_part, in_=block_part, compare_op=ALU.is_ge, fill=0.0, base=0,
                                           pattern=[[0, HG], [1, P]], channel_multiplier=-1).then_inc(sg.probs_masked, 1)
                    if squared:
                        roots(at[g, st])
                    else:
                        if n:
                            add(n - 1, 0)
                        roots(at[g, st])
                        if n:
                            add(n - 1, 1)
                if not squared:
                    add(NG * NSTEPS - 1, 0)
                    add(NG * NSTEPS - 1, 1)
                if mqa:
                    for t in range(NT):
                        pool.wait_ge(sg.tile_in[t % 4], tiles_before + DMA * (t // 4 + 1))
                        x = s["tiles"][:, t % 4, :]
                        pool.tensor_tensor(x, x, w["bo"][:], ALU.add).then_inc(sg.biased, 1)

        @block.scalar
        def _(act):
            features = Count()
            shifts = [Count() for c in range(NC)]

            def high(name, out, source, bias=None):
                wait_work(act, name)
                if bias is None:
                    ins = act.activation(out, source, ACT.Copy)
                else:
                    ins = act.activation(out, source, ACT.Identity, bias=bias)
                ins.then_inc(sg.work_high[bank(name)], 1)

            def take(name):
                u = name[0]
                if u == "ln":
                    t = name[1]
                    high(name, s["xnT"][:, HIGH, :, P * t:P * t + P],
                         work[:, bank(name), :].rearrange("p (kc q) -> p kc q", kc=KC))
                    if t + 4 < NT:
                        load(act, t + 4, b + 1)
                elif u in ("ks", "kt"):
                    c = name[1]
                    high(name, s["k"][0:STACK, 1, CHUNK * c:CHUNK * c + CHUNK], work[0:STACK, bank(name), :],
                         w["bk"][:, 0:1] if mqa else None)
                elif u == "gate_exp":
                    act.wait_ge(sg.gate_shifted, 1)
                    act.activation(s["gate_exp"][:], s["logits"][:], ACT.Exp).then_inc(sg.gate_exp, 1)
                elif u == "q" and not squared:
                    _, g, c = name
                    wait_pair_free(act, name)
                    high(name, s["pair"][:, c, HIGH, :], work[:, bank(name), :],
                         w["bq"][:, g % NG:g % NG + 1] if mqa else None)
                elif u == "max":
                    c = name[2]
                    if shifts[c].next():
                        act.wait_ge(sg.shift_moved[c], DMA * 2 * (shifts[c].n - 1))
                    high(name, s["shift"][:, c, HIGH, :], work[0:HG * TPC, bank(name), 0:P])
                elif u in ("q", "k"):
                    n = features.next()
                    wait_work(act, name)
                    if n >= 2:
                        act.wait_ge(sg.low_done[n % 2], n // 2)
                    act.activation(s["centred"][:, n % 2, :], work[:, bank(name), :], ACT.Identity,
                                   bias=w["feature_bias"][:, 0:1]).then_inc(sg.centred, 1)
                    if n:
                        last = feature_units[n - 1]
                        wait_work(act, (last[0] + "col", *last[1:]))
                    act.activation(s["squares"][:], work[:, bank(name), :], ACT.Square,
                                   bias=w["feature_bias"][:, 0:1]).then_inc(sg.work_free[bank(name)], 1)
                elif u == "sums":
                    m = name[1]
                    if m:
                        wait_work(act, ("sumcol", m - 1))
                    if squared:
                        act.wait_ge(sg.summed, end_of(m))
                        act.activation(s["sums"][:], sums_bank, ACT.Identity, bias=k["eps"][:, 0:1]).then_inc(sg.sums_copied, 1)
                    else:
                        wait_work(act, name)
                        act.activation(s["sums"][:], work[:, bank(name), :], ACT.Copy).then_inc(sg.work_free[bank(name)], 1)
                elif u in ("qwide", "kwide", "sumwide"):
                    wait_free(act, (u.replace("wide", "col"), *name[1:]))
                    n = wide_events.index(name)
                    if n:
                        last = wide_events[n - 1]
                        wait_work(act, (last[0].replace("wide", "row"), *last[1:]))
                    act.activation(s["wide_inverse"][:].rearrange("p (t i d) -> p t i d", i=HG, d=D),
                                   s["inverse"][:, :, :, None].broadcast_to([P, TPC, HG, D]), ACT.Copy)\
                        .then_inc(sg.widened, 1)
                elif u in ("qvar", "kvar"):
                    wait_work(act, name)
                    act.activation(s["squares"][:], work[:, bank(name), :], ACT.Sqrt,
                                   bias=k["eps"][:, 0:1]).then_inc(sg.work_free[bank(name)], 1)

            if not attends:
                for name in events:
                    take(name)
                return

            def probs(n, x):
                st = n % NSTEPS
                off, number = offset(st), scores_before[n] + x
                i, many = parts_of(st)[x]
                act.wait_ge(sg.scores_ready, number + 1)
                act.activation(probs_of(n)[:, i:i + many, off:],
                               score_banks[:, number % nbanks, 0:many * (CHUNK - off)].rearrange("p (i q) -> p i q", i=many),
                               ACT.Square if squared else ACT.Exp, scale=SCALE).then_inc(sg.probs_ready, 1)

            def copy_heads(m):
                g, c = divmod(m, NC)
                act.wait_ge(sg.values_done, end_of(m))
                act.activation(s["y"][:, g, CHUNK * c:CHUNK * c + CHUNK], heads[:], ACT.Copy)\
                    .then_inc(sg.heads_copied, 1)

            for n in range(NG * NSTEPS):
                g, st = divmod(n, NSTEPS)
                c, kb = STEPS[st]
                if kb == 0 and not squared:
                    if g:
                        wait_work(act, ("sums", NC * (g - 1) + c))
                elif ring(n) >= slots:
                    old = next(o for o in range(n) if ring(o) == ring(n) - slots and (squared or STEPS[o % NSTEPS][1]))
                    if squared:
                        act.wait_ge(sg.summed, old + 1)
                    else:
                        act.wait_ge(sg.values_done, old + 1)
                        act.wait_ge(sg.added, 2 * (ring(old) + 1))
                banks = range(len(parts_of(st)))
                for x in banks[:2]:
                    probs(n, x)
                for name in at[g, st]:
                    take(name)
                for m in range(NC * NG - 1):
                    if n == end_of(m):
                        copy_heads(m)
                for x in banks[2:]:
                    probs(n, x)
            copy_heads(NC * NG - 1)
            for name in tail[:4]:
                take(name)

        @block.vector
        def _(dve):
            steps, features, pieces, widened = Count(), Count(), Count(), Count()

            def then(ins):
                ins.then_inc(sg.vector_step, 1)
                dve.wait_ge(sg.vector_step, steps.next() + 1)

            def low(name, out, source, high_part, bias=None):
                wait_high(dve, name)
                if bias is None:
                    ins = dve.tensor_tensor(out, source, high_part.bitcast(F32), ALU.subtract)
                else:
                    ins = dve.scalar_tensor_tensor(out, source, bias, high_part.bitcast(F32), ALU.add, ALU.subtract)
                ins.then_inc(sg.work_free[bank(name)], 1)

            def each(x):
                return x[:, :, None].broadcast_to([P, NT, HEADS])

            def gate(name):
                wait_work(dve, name)
                gl = work[:, bank(name), 0:NT * HEADS].rearrange("p (t h) -> p t h", t=NT)
                then(dve.reduce_max(s["logit_max"][:], gl, AX_X))
                dve.tensor_tensor(s["logits"][:], gl, each(s["logit_max"]), ALU.subtract)\
                    .then_inc(sg.work_free[bank(name)], 1)
                wait_free(dve, name)
                dve.tensor_single_scalar(s["is_max"][:], s["logits"][:], 0.0, ALU.is_equal).then_inc(sg.gate_shifted, 1)
                dve.wait_ge(sg.gate_shifted, 1)
                then(dve.tensor_tensor(s["is_max"][:], s["is_max"][:], k["rank"][:], ALU.mult))
                then(dve.reduce_max(s["best"][:], s["is_max"][:], AX_X))
                then(dve.tensor_tensor(s["chosen"][:], k["rank"][:], each(s["best"]), ALU.is_equal))

            def gate_value():
                dve.wait_ge(sg.gate_exp, 1)
                then(dve.reduce_sum(s["exp_sum"][:], s["gate_exp"][:], AX_X))
                then(dve.reciprocal(s["top"][:], s["exp_sum"][:]))
                then(dve.tensor_tensor(s["gate"][:], s["chosen"][:], each(s["top"]), ALU.mult))

            def select(name, n, pick, out):
                t = name[1]
                wait_work(dve, name)
                dve.tensor_tensor(s["masked"][:, n, :].rearrange("p (h d) -> p h d", h=HEADS),
                                  work[:, bank(name), :].rearrange("p (h d) -> p h d", h=HEADS),
                                  s[pick][:, t, :][:, :, None].broadcast_to([P, HEADS, D]), ALU.mult)\
                    .then_inc(sg.work_free[bank(name)], 1)
                wait_free(dve, name)
                return dve.tensor_reduce(out, s["masked"][:, n, :].rearrange("p (h d) -> p d h", h=HEADS), AX_X, ALU.add)

            def piece(g, j):
                t, p, width, i, many = PIECES[j]
                n = pieces.next()
                if n == 0 and part == "first":
                    dve.wait_ge(sg.built, 2)
                dve.wait_ge(sg.piece_ready, n + 1)
                dve.reduce_max(s["maxima"][:, g % 2, i:i + many, t, p],
                               piece_banks[:, n % 2, 0:many * width].rearrange("p (i k) -> p i k", i=many), AX_X)\
                    .then_inc(sg.piece_used, 1)

            def take(name):
                u = name[0]
                if u == "pieces":
                    for j in range(*name[2:]):
                        piece(name[1], j)
                elif u == "stats":
                    t = name[1]
                    dve.wait_ge(sg.tile_in[t % 4], DMA * (t // 4 + 1))
                    then(dve.bn_stats(s["stats"][:, t, :], s["tiles"][:, t % 4, :]))
                    then(dve.bn_aggr(s["mean_var"][:, t, :], s["stats"][:, t, :]))
                    dve.tensor_scalar(s["var_eps"][:, t:t + 1], s["mean_var"][:, t, 1:2], EPS, None, ALU.add)\
                        .then_inc(sg.variance, 1)
                elif u == "norm":
                    t = name[1]
                    dve.wait_ge(sg.rstd, t + 1)
                    x = s["tiles"][:, t % 4, :]
                    dve.tensor_scalar(x, x, s["mean_var"][:, t, 0:1], s["rstd"][:, t:t + 1], ALU.subtract,
                                      ALU.mult).then_inc(sg.normed, 1)
                elif u == "ln":
                    cols = slice(P * name[1], P * name[1] + P)
                    low(name, s["xnT"][:, LOW, :, cols], work[:, bank(name), :].rearrange("p (kc q) -> p kc q", kc=KC),
                        s["xnT"][:, HIGH, :, cols])
                elif u in ("ks", "kt"):
                    rest = s["k"][2 * D:STACK, 1, CHUNK * name[1]:CHUNK * name[1] + CHUNK]
                    low(name, rest, work[2 * D:STACK, bank(name), :], rest, w["bk"][2 * D:STACK, 0:1] if mqa else None)
                elif u == "vs":
                    wait_work(dve, name)
                    dve.tensor_tensor(s["v"][:, 1], work[:, bank(name), 0:NT * D].rearrange("p (t d) -> p t d", t=NT),
                                      w["bv"][:, None, :].broadcast_to([P, NT, D]), ALU.add)\
                        .then_inc(sg.work_free[bank(name)], 1)
                elif u == "gate":
                    gate(name)
                elif u == "gate_value":
                    gate_value()
                elif u == "kall":
                    t = name[1]
                    then(select(name, 0, "chosen", s["k_token"][:, t, 0:D]))
                    dve.tensor_copy(s["k_token"][:, t, D:STACK].rearrange("p (r d) -> p r d", d=D),
                                    s["k_token"][:, t, 0:D][:, None, :].broadcast_to([P, 2, D])).then_inc(sg.selected, 1)
                elif u == "vall":
                    then(select(name, 1, "gate", s["v"][:, 1, name[1], :]))
                elif u == "v":
                    _, g, half = name
                    wait_work(dve, name)
                    dve.tensor_copy(s["v"][:, g % 2, TPC * half:TPC * half + TPC, :],
                                    work[:, bank(name), :].rearrange("p (t d) -> p t d", t=TPC))\
                        .then_inc(sg.work_free[bank(name)], 1)
                elif u == "q" and not squared:
                    _, g, c = name
                    low(name, s["pair"][:, c, LOW, :], work[:, bank(name), :], s["pair"][:, c, HIGH, :],
                        w["bq"][:, g % NG:g % NG + 1] if mqa else None)
                elif u == "maxred":
                    _, g, c = name
                    if pieces.n:
                        dve.wait_ge(sg.piece_used, pieces.n)
                    dve.tensor_reduce(s["minus_max"][:, c, :].rearrange("p (i t) -> p i t", i=HG),
                                      s["maxima"][:, g % 2, :, TPC * c:TPC * c + TPC, :],
                                      AX_X, ALU.max, negate=True).then_inc(sg.max_ready, 1)
                elif u == "max":
                    c = name[2]
                    low(name, s["shift"][:, c, LOW, :], work[0:HG * TPC, bank(name), 0:P], s["shift"][:, c, HIGH, :])
                elif u in ("qcol", "kcol", "sumcol"):
                    wait_work(dve, name)
                    if widened.next():
                        dve.wait_ge(sg.widened, widened.n - 1)
                    dve.reciprocal(s["inverse"][:], work[:, bank(name), :].rearrange("p (t i d) -> p t i d", i=HG, d=D)[:, :, :, 0])\
                        .then_inc(sg.work_free[bank(name)], 1)
                elif u == "sumrow":
                    g, c = divmod(name[1], NC)
                    out = s["y"][:, g, CHUNK * c:CHUNK * c + CHUNK]
                    wait_work(dve, name)
                    dve.wait_ge(sg.heads_copied, name[1] + 1)
                    dve.tensor_tensor(out, work[:, bank(name), :], out, ALU.mult).then_inc(sg.work_free[bank(name)], 1)
                elif u in ("qrow", "krow"):
                    _, g, c = name
                    n = features.next()
                    stacked = (u[0], g, c)
                    centred, pair = s["centred"][:, n % 2, :], s["pair"][:, c]
                    wait_work(dve, name)
                    dve.wait_ge(sg.centred, n + 1)
                    dve.tensor_tensor(centred, work[:, bank(name), :], centred, ALU.mult)\
                        .then_inc(sg.work_free[bank(name)], 1)
                    wait_free(dve, name)
                    wait_pair_free(dve, stacked)
                    then(dve.tensor_copy(pair[:, HIGH, :], centred))
                    dve.tensor_tensor(pair[:, LOW, :], centred, pair[:, HIGH, :].bitcast(F32),
                                      ALU.subtract).then_inc(sg.low_done[c], 1)

            if not attends:
                for name in events:
                    take(name)
                return

            if not squared:
                dve.tensor_copy(s["k"][0:SHIFT, 0, :], s["k"][0:SHIFT, 1, :].bitcast(F32)).then_inc(sg.brought, 1)
                dve.tensor_copy(s["v"][:, 0], s["v"][:, 1]).then_inc(sg.brought, 1)

            for n in range(NG * NSTEPS):
                g, st = divmod(n, NSTEPS)
                mine = pieces_at(kind, part, g, st)
                for j in mine[:1]:
                    piece(g + 1, j)
                for name in at[g, st]:
                    take(name)
                for j in mine[1:]:
                    piece(g + 1, j)

            def add_residual(t):
                name = ("out", t)
                x = s["tiles"][:, t % 4, :]
                wait_work(dve, name)
                if mqa:
                    dve.wait_ge(sg.biased, t + 1)
                else:
                    dve.wait_ge(sg.tile_in[t % 4], tiles_before + DMA * (t // 4 + 1))
                dve.tensor_tensor(x, work[:, bank(name), :], x, ALU.add).then_inc(sg.work_free[bank(name)], 1)

            for name in tail[:4]:
                take(name)
            for t in range(NT):
                add_residual(t)

        @block.tensor
        def _(pe):
            pieces, diagonals, normed, widened = Count(), Count(), Count(), Count()
            known = set()

            def free(name):
                if unit[name] >= 2:
                    pe.wait_ge(sg.work_free[bank(name)], unit[name] // 2)
                return work[:, bank(name), :]

            def ready(name, ins):
                ins.then_inc(sg.work_ready[bank(name)], 1)

            def xn(a, kc, cols):
                return s["xnT"][:, a, kc, cols]

            def need_tiles(tiles):
                for t in tiles:
                    if t not in known:
                        known.add(t)
                        wait_free(pe, ("ln", t))

            def token_product(out, t, weight, cols):
                return pair_product(pe, out, lambda a, kc: xn(a, kc, slice(P * t, P * t + P)),
                                    lambda a, kc: w[weight][:, a, kc, cols])

            def channel_product(out, c, weight, cols):
                return pair_product(pe, out, lambda a, kc: w[weight][:, a, kc, cols],
                                    lambda a, kc: xn(a, kc, slice(CHUNK * c, CHUNK * c + CHUNK)))

            def piece(g, j):
                t, p, width, i, many = PIECES[j]
                n = pieces.next()
                diagonal = P * (t + 1) <= CHUNK * (p + 1)
                if j == 0:
                    wait_stack(pe, ("q", g, 0))
                    if g >= NG:
                        if part == "first":
                            pe.wait_ge(sg.built, 2)
                        wait_free(pe, ("ks" if mqa else "kt", 0))
                if j == SECOND_HALF:
                    wait_stack(pe, ("q", g, 1))
                    if g >= NG:
                        wait_free(pe, ("ks" if mqa else "kt", 1))
                if n >= 2:
                    pe.wait_ge(sg.piece_used, n - 1)
                for x in range(many):
                    out = piece_banks[:, n % 2, width * x:width * x + width]
                    ins = pe.matmul(out, s["q"][0:STACK, g % 2, t // TPC, i + x, P * (t % TPC):P * (t % TPC) + P],
                                    s["k"][0:STACK, keys_of(g), CHUNK * p:CHUNK * p + width], start=True, stop=not diagonal)
                    if diagonal:
                        ins = pe.matmul(out[:, width - P:width], k["ident16"][:], k["mask"][:], start=False, stop=True)
                ins.then_inc(sg.piece_ready, 1)

            def take(name):
                u = name[0]
                if u == "pieces":
                    for j in range(*name[2:]):
                        piece(name[1], j)
                elif u == "ln":
                    t = name[1]
                    pe.wait_ge(sg.normed, t + 1)
                    out = free(name)
                    for kc in range(KC):
                        ins = pe.transpose(tile_of(out, kc), tile_of(s["tiles"][:, t % 4, :], kc), k["ident"][:])
                    ready(name, ins)
                elif u == "ks":
                    c = name[1]
                    need_tiles(range(TPC * c, TPC * c + TPC))
                    ready(name, channel_product(free(name)[0:STACK, :], c, "wk", slice(0, STACK)))
                elif u == "vs":
                    need_tiles(range(NT))
                    out = free(name)
                    for t in range(NT):
                        ins = token_product(out[:, D * t:D * t + D], t, "wv", slice(0, D))
                    ready(name, ins)
                elif u == "gate":
                    need_tiles(range(NT))
                    out = free(name)
                    for t in range(NT):
                        ins = token_product(out[:, HEADS * t:HEADS * t + HEADS], t, "wg", slice(0, HEADS))
                    ready(name, ins)
                elif u in ("kall", "vall"):
                    ready(name, token_product(free(name), name[1], "wk" if u == "kall" else "wv", slice(0, C)))
                elif u == "kt":
                    out = free(name)
                    for t in range(TPC):
                        pe.wait_ge(sg.selected, TPC * name[1] + t + 1)
                        ins = pe.transpose(tile_of(out, t)[0:STACK, :], s["k_token"][:, TPC * name[1] + t, :], k["ident"][:])
                    ready(name, ins)
                elif u == "max":
                    pe.wait_ge(sg.max_ready, normed.next() + 1)
                    out = free(name)
                    ready(name, pe.transpose(out[0:HG * TPC, 0:P], s["minus_max"][:, name[2], :], k["ident"][:]))
                elif u in ("q", "k"):
                    _, g, c = name
                    if g >= NG:
                        need_tiles(range(TPC * c, TPC * c + TPC))
                    ready(name, channel_product(free(name), c, "w" + u, slice(P * (g % NG), P * (g % NG) + P)))
                elif u == "v":
                    _, g, half = name
                    if g >= NG:
                        need_tiles(range(TPC * half, TPC * half + TPC))
                    out = free(name)
                    for t in range(TPC):
                        ins = token_product(tile_of(out, t), TPC * half + t, "wv", slice(P * (g % NG), P * (g % NG) + P))
                    ready(name, ins)
                elif u == "sums" and not squared:
                    m = name[1]
                    out = free(name)
                    pe.wait_ge(sg.added, 2 * (end_of(m) - m - 1))
                    for i in range(HG):
                        ins = pe.matmul(out[D * i:D * i + D, :], k["ones"][:], s["first_probs"][:, m % NC, i, :],
                                        start=True, stop=True)
                    ready(name, ins)
                elif u in ("qcol", "kcol", "sumcol"):
                    if u == "sumcol":
                        source_rows = s["sums"]
                        if squared:
                            pe.wait_ge(sg.sums_copied, name[1] + 1)
                        else:
                            wait_free(pe, ("sums", name[1]))
                    else:
                        source_rows = s["squares"]
                        wait_free(pe, (u[0] + "var", *name[1:]))
                    out = free(name)
                    for t in range(TPC):
                        ins = pe.transpose(tile_of(out, t), tile_of(source_rows, t), k["ident"][:])
                    ready(name, ins)
                elif u in ("qrow", "krow", "sumrow"):
                    pe.wait_ge(sg.widened, widened.next() + 1)
                    out = free(name)
                    for t in range(TPC):
                        ins = pe.transpose(tile_of(out, t), tile_of(s["wide_inverse"], t), k["ident"][:])
                    ready(name, ins)
                elif u in ("qvar", "kvar"):
                    wait_free(pe, (u[0], *name[1:]))
                    ready(name, pe.matmul(free(name), k["head_mean"][:].rearrange("p i d -> p (i d)"), s["squares"][:],
                                          start=True, stop=True))

            if not attends:
                for name in events:
                    take(name)
                return

            def scores(n, x):
                g, st = divmod(n, NSTEPS)
                c, kb = STEPS[st]
                off, number = offset(st), scores_before[n] + x
                first, many = parts_of(st)[x]
                if number >= nbanks:
                    pe.wait_ge(sg.probs_ready, number - nbanks + 1)
                diagonal = kb >= TPC * c and not squared
                width = CHUNK - off
                for y in range(many):
                    i = first + y
                    out = score_banks[:, number % nbanks, width * y:width * y + width]
                    keys = s["k"][0:rows, g % 2, i, P * kb:P * kb + P] if squared else s["k"][0:rows, 0, P * kb:P * kb + P]
                    ins = pe.matmul(out, keys, s["q"][0:rows, g % 2, c, i, off:],
                                    start=True, stop=not diagonal)
                    if diagonal:
                        ins = pe.matmul(out[:, 0:P], k["ident16"][:], k["mask_t"][:], start=False, stop=True)
                ins.then_inc(sg.scores_ready, 1)

            def value_products(n):
                g, st = divmod(n, NSTEPS)
                c, kb = STEPS[st]
                off = max(P * (kb - TPC * c), 0)
                if n == 0 and not squared:
                    pe.wait_ge(sg.brought, 2)
                pe.wait_ge(sg.probs_ready, scores_before[n + 1])
                if squared and kb >= TPC * c:
                    pe.wait_ge(sg.probs_masked, diagonals.next() + 1)
                if kb == 0 and NC * g + c:
                    pe.wait_ge(sg.heads_copied, NC * g + c)
                for i in range(HG):
                    left = s["v"][:, g % 2, kb, D * i:D * i + D] if squared else s["v"][:, 0, kb, :]
                    ins = pe.matmul(heads[D * i:D * i + D, off:], left, probs_of(n)[:, i, off:],
                                    start=(kb == 0), stop=(kb == TPC * (c + 1) - 1))
                ins.then_inc(sg.values_done, 1)

            def step_sums(n):
                g, st = divmod(n, NSTEPS)
                c, kb = STEPS[st]
                off = max(P * (kb - TPC * c), 0)
                if kb == 0 and NC * g + c:
                    pe.wait_ge(sg.sums_copied, NC * g + c)
                for i in range(HG):
                    ins = pe.matmul(sums_bank[D * i:D * i + D, off:], k["ones"][:], probs_of(n)[:, i, off:],
                                    start=(kb == 0), stop=(kb == TPC * (c + 1) - 1))
                ins.then_inc(sg.summed, 1)

            if not squared:
                pe.wait_ge(sg.brought, 1)
            for g in range(NG):
                for st in range(NSTEPS):
                    n = g * NSTEPS + st
                    mine = pieces_at(kind, part, g, st)
                    if st in CHUNK_STEPS:
                        wait_stack(pe, ("q", g, STEPS[st][0]))
                        if not squared and (g or st):
                            pe.wait_ge(sg.shift_moved[STEPS[st][0]], DMA * 2 * (g if st == 0 else g + 1))
                        if squared:
                            wait_stack(pe, ("k", g, STEPS[st][0]))

                    def some(a, z=None):
                        for j in mine[a:z]:
                            piece(g + 1, j)

                    banks = range(len(parts_of(st)))
                    scores(n, 0)
                    some(0, 1)
                    for x in banks[1:2]:
                        scores(n, x)
                    for name in at[g, st]:
                        take(name)
                    some(1, 2)
                    if squared:
                        for x in banks[2:]:
                            scores(n, x)
                    if n:
                        value_products(n - 1)
                        if squared:
                            step_sums(n - 1)
                    some(2, 3)
                    for x in [] if squared else banks[2:3]:
                        scores(n, x)
                    some(3, 4)
                    for x in [] if squared else banks[3:]:
                        scores(n, x)
                    some(4)
            value_products(NG * NSTEPS - 1)
            if squared:
                step_sums(NG * NSTEPS - 1)
            for name in tail[:4]:
                take(name)
            for m in range(NC * NG):
                if m >= NC * NG - 2:
                    wait_free(pe, ("sumrow", m))
            for t in range(NT):
                name = ("out", t)
                out = free(name)
                for g in range(NG):
                    if gated:
                        ins = pe.transpose(tile_of(out, g), out_view(t)[:, g, :], k["ident"][:])
                    else:
                        ins = pe.matmul(out, out_view(t)[:, g, :], w["wo"][:, g, :], start=(g == 0), stop=(g == NG - 1))
                ready(name, ins)


def build(nc, dram, out):
    with ExitStack() as ctx:
        sg = Signals(nc, ctx)
        psum = ctx.enter_context(nc.psum_tensor("banks", [P, 8, CHUNK], F32))
        k = make_constants(nc, ctx, sg)
        for layer, kind in enumerate(LAYERS):
            with ExitStack() as own:
                def pair(name, n):
                    return own.enter_context(nc.sbuf_tensor(f"{name}_{layer}", [P, 2, KC, n], F32R))

                def plain(name, shape):
                    return own.enter_context(nc.sbuf_tensor(f"{name}_{layer}", shape, F32))

                w = {"wq": pair("wq", C)}
                if kind == "squared":
                    w |= {"wk": pair("wk", C), "wv": pair("wv", C), "wo": plain("wo", [P, KC, C]),
                          "feature_bias": plain("feature_bias", [P, 1])}
                    prepare_squared(nc, sg, k, psum, w, dram["squared"])
                elif kind == "gated":
                    w |= {"wk": pair("wk", C), "wv": pair("wv", C), "wg": pair("wg", HEADS)}
                    prepare_gated(nc, sg, k, psum, w, dram["gated"], layer)
                else:
                    w |= {"wk": pair("wk", STACK), "wv": pair("wv", D), "wo": plain("wo", [P, KC, C]),
                          "bq": plain("bq", [P, NG]), "bk": plain("bk", [STACK, 1]), "bv": plain("bv", [P, D]),
                          "bo": plain("bo", [P, C])}
                    w |= {f"wk{r}": w["wk"][:, :, :, D * r:D * r + D] for r in range(3)}
                    prepare_mqa(nc, sg, k, psum, w, dram["mqa"])
                s = stage_buffers(nc, own, kind, layer)
                source = dram["x"] if layer == 0 else out
                stage(nc, sg, k, psum, w, s, kind, "first", -1, source, out)
                nc.all_engine_barrier(sems_to_clear=sg.range)
                if B > 1:
                    with nc.Fori(0, B - 1) as b:
                        stage(nc, sg, k, psum, w, s, kind, "middle", b, source, out)
                        nc.all_engine_barrier(sems_to_clear=sg.range)
                stage(nc, sg, k, psum, w, s, kind, "last", B - 1, source, out)
                nc.all_engine_barrier(sems_to_clear=sg.range)


def kernel(**inputs):
    import numpy as np
    import concourse.bacc as bacc
    from concourse.bass_utils import run_bass_kernel_spmd

    def a(name):
        return np.asarray(inputs[f"L0_{name}"])

    arrays = {
        "x": a("attn_a_hidden_states"),
        "squared_wq": a("attn_a_Wq"), "squared_wk": a("attn_a_Wk"), "squared_wvT": a("attn_a_Wv").T,
        "squared_woT": a("attn_a_Wo").T, "squared_gamma": a("attn_a_gamma"), "squared_beta": a("attn_a_beta"),
        "mqa_wqkvT": a("attn_b_Wqkv_w").T, "mqa_bqkv": a("attn_b_Wqkv_b"),
        "mqa_woT": a("attn_b_out_w").T, "mqa_bout": a("attn_b_out_b"),
        "gated_wgateT": a("ffn_W_gate").T, "gated_wqkvT": a("ffn_W_qkv").T,
    }
    arrays = {f"in_{n}": np.ascontiguousarray(v) for n, v in arrays.items()}
    nc = bacc.Bacc("TRN2", target_bir_lowering=False, num_devices=1, dynamic_dma_scratch_size=1024)
    aps = {n: nc.dram_tensor(n, v.shape, F32, kind="ExternalInput").ap() for n, v in arrays.items()}
    dram = {"x": aps["in_x"]}
    for kind in ("squared", "gated", "mqa"):
        start = f"in_{kind}_"
        dram[kind] = {n[len(start):]: ap for n, ap in aps.items() if n.startswith(start)}
    out = nc.dram_tensor("out", (B, T, C), F32, kind="ExternalOutput").ap()
    build(nc, dram, out)
    result = run_bass_kernel_spmd(nc, [arrays], core_ids=[0])
    return result.results[0]["out"]
```
